# Optimizing a Trainium2 kernel written in Bass

```python
import numpy as np
import jax
import jax.numpy as jnp

def _softmax(x, axis=-1):
    return jax.nn.softmax(x, axis=axis)

def _gelu(x):
    return jax.nn.gelu(x, approximate=True)

def _silu(x):
    return jax.nn.silu(x)

def _sigmoid(x):
    return jax.nn.sigmoid(x)

def _layernorm(x, axis=-1, eps=1e-05):
    m = jnp.mean(x, axis=axis, keepdims=True)
    v = jnp.var(x, axis=axis, keepdims=True)
    return (x - m) / jnp.sqrt(v + eps)

def _scatter_add(tgt, idx, src, axis=0):
    return tgt.at[idx].add(src)

def _segment_sum(src, seg, n):
    return jax.ops.segment_sum(src, seg, n)
kernel_name = 'mk_metaformer_d1_conv_nhwc1024_r4_0f139f'

def setup_inputs(seed: int=0):
    np.random.seed(seed)
    _w = jnp.asarray

    def _rec_inputs():
        import jax
        import jax.numpy as jnp
        _gk = jax.random.key(seed)
        x = -0.000125 + 0.9999 * jax.random.normal(jax.random.fold_in(_gk, 1), (8, 16, 16, 256), jnp.float32)
        return x
    x = _rec_inputs()

    def _L0_conv_setup():
        import jax, jax.numpy as jnp
        import numpy as np
        B, H, W, D = (8, 16, 16, 256)

        def _dist(n, dtype):
            i = jnp.arange(n)
            return jnp.square(i[:, None] - i[None, :]).astype(dtype)
        key = jax.random.key(seed)
        ks = jax.random.split(key, 10)
        s = 0.02
        return {'x': jax.random.normal(ks[0], (B, H, W, D), dtype=jnp.float32), 'Wq': jax.random.normal(ks[1], (D, D), dtype=jnp.float32) * s, 'bq': jnp.zeros((D,), dtype=jnp.float32), 'Wk': jax.random.normal(ks[2], (D, D), dtype=jnp.float32) * s, 'bk': jnp.zeros((D,), dtype=jnp.float32), 'Wv': jax.random.normal(ks[3], (D, D), dtype=jnp.float32) * s, 'bv': jnp.zeros((D,), dtype=jnp.float32), 'Wo': jax.random.normal(ks[4], (D, D), dtype=jnp.float32) * s, 'bo': jnp.zeros((D,), dtype=jnp.float32), 'sigma': jnp.ones((1,), dtype=jnp.float32)}
    _L0_conv_all = _L0_conv_setup()
    _L0_conv_in = {k: v for k, v in _L0_conv_all.items() if k in ('Wq', 'bq', 'Wk', 'bk', 'Wv', 'bv', 'Wo', 'bo', 'sigma')}
    del _L0_conv_all

    def _L0_ffn_setup():
        import jax, jax.numpy as jnp
        import numpy as np
        CAPACITY_FACTOR = 1.0

        def _top1_gate(x2d, wg):
            S, _ = x2d.shape
            E = wg.shape[1]
            C = int(CAPACITY_FACTOR * S / E)
            logits = x2d @ wg
            gates = jax.nn.softmax(logits, axis=-1)
            idx = jnp.argmax(gates, axis=-1)
            mask = jax.nn.one_hot(idx, E, dtype=jnp.int32)
            loc = jnp.cumsum(mask, axis=0) - 1
            me = jnp.mean(gates, axis=0)
            ce = jnp.mean(mask.astype(gates.dtype), axis=0)
            l_aux = E * jnp.sum(me * ce)
            mask = mask * (loc < C).astype(jnp.int32)
            gate_s = jnp.sum(gates * mask, axis=-1)
            loc_s = jnp.sum(loc * mask, axis=-1)
            loc_oh = jax.nn.one_hot(loc_s, C, dtype=gates.dtype)
            combine = (gate_s[:, None] * mask.astype(gates.dtype))[:, :, None] * loc_oh[:, None, :]
            dispatch = (combine > 0).astype(gates.dtype)
            return (l_aux, combine, dispatch)
        key = jax.random.key(seed)
        k1, k2, k3, k4 = jax.random.split(key, 4)
        s, b, m, E, ffn = (512, 4, 256, 8, 1024)
        x = jax.random.normal(k1, (s, b, m), dtype=jnp.float32)
        wg = jax.random.normal(k2, (m, E), dtype=jnp.float32) * 0.02
        w1 = jax.random.normal(k3, (E, m, ffn), dtype=jnp.float32) * 0.02
        w2 = jax.random.normal(k4, (E, ffn, m), dtype=jnp.float32) * 0.02
        return {'x': x, 'wg': wg, 'w1': w1, 'w2': w2}
    _L0_ffn_all = _L0_ffn_setup()
    _L0_ffn_in = {k: v for k, v in _L0_ffn_all.items() if k in ('wg', 'w1', 'w2')}
    del _L0_ffn_all
    return {'x': x, 'L0_conv_Wq': _L0_conv_in['Wq'], 'L0_conv_bq': _L0_conv_in['bq'], 'L0_conv_Wk': _L0_conv_in['Wk'], 'L0_conv_bk': _L0_conv_in['bk'], 'L0_conv_Wv': _L0_conv_in['Wv'], 'L0_conv_bv': _L0_conv_in['bv'], 'L0_conv_Wo': _L0_conv_in['Wo'], 'L0_conv_bo': _L0_conv_in['bo'], 'L0_conv_sigma': _L0_conv_in['sigma'], 'L0_ffn_wg': _L0_ffn_in['wg'], 'L0_ffn_w1': _L0_ffn_in['w1'], 'L0_ffn_w2': _L0_ffn_in['w2']}

def reference(x, L0_conv_Wq, L0_conv_bq, L0_conv_Wk, L0_conv_bk, L0_conv_Wv, L0_conv_bv, L0_conv_Wo, L0_conv_bo, L0_conv_sigma, L0_ffn_wg, L0_ffn_w1, L0_ffn_w2):
    import jax
    import jax.numpy as jnp

    def _L0_conv_ref(x, Wq, bq, Wk, bk, Wv, bv, Wo, bo, sigma):
        import jax, jax.numpy as jnp
        import numpy as np
        B, H, W, D = (8, 16, 16, 256)

        def _dist(n, dtype):
            i = jnp.arange(n)
            return jnp.square(i[:, None] - i[None, :]).astype(dtype)
        b, h, w, d = x.shape
        gw = 1.0 / (2.0 * jnp.square(sigma))
        q = jnp.einsum('bhwd,ed->bhwe', x, Wq) + bq
        k = jnp.einsum('bhwd,ed->bhwe', x, Wk) + bk
        v = jnp.einsum('bhwd,ed->bhwe', x, Wv) + bv
        r_qk = jnp.einsum('bhwd,bhkd->bhwk', q, k) - gw[0] * _dist(w, x.dtype)
        r_attn = jax.nn.softmax(r_qk, axis=-1)
        r_out = jnp.einsum('bhwk,bhkd->bhwd', r_attn, v)
        c_qk = jnp.einsum('bhwd,bgwd->bwhg', q, k) - gw[0] * _dist(h, x.dtype)
        c_attn = jax.nn.softmax(c_qk, axis=-1)
        c_out = jnp.einsum('bwhg,bgwd->bhwd', c_attn, v)
        out = r_out + c_out
        return jnp.einsum('bhwd,ed->bhwe', out, Wo) + bo

    def _L0_ffn_ref(x, wg, w1, w2):
        import jax, jax.numpy as jnp
        import numpy as np
        CAPACITY_FACTOR = 1.0

        def _top1_gate(x2d, wg):
            S, _ = x2d.shape
            E = wg.shape[1]
            C = int(CAPACITY_FACTOR * S / E)
            logits = x2d @ wg
            gates = jax.nn.softmax(logits, axis=-1)
            idx = jnp.argmax(gates, axis=-1)
            mask = jax.nn.one_hot(idx, E, dtype=jnp.int32)
            loc = jnp.cumsum(mask, axis=0) - 1
            me = jnp.mean(gates, axis=0)
            ce = jnp.mean(mask.astype(gates.dtype), axis=0)
            l_aux = E * jnp.sum(me * ce)
            mask = mask * (loc < C).astype(jnp.int32)
            gate_s = jnp.sum(gates * mask, axis=-1)
            loc_s = jnp.sum(loc * mask, axis=-1)
            loc_oh = jax.nn.one_hot(loc_s, C, dtype=gates.dtype)
            combine = (gate_s[:, None] * mask.astype(gates.dtype))[:, :, None] * loc_oh[:, None, :]
            dispatch = (combine > 0).astype(gates.dtype)
            return (l_aux, combine, dispatch)
        s, b, m = x.shape
        x2d = x.reshape(-1, m)
        l_aux, combine, dispatch = _top1_gate(x2d, wg)
        combine = combine[:, None]
        dispatch = dispatch[:, None]
        xr = x2d[:, None, :]
        dispatched = jnp.einsum('szfc,szm->zfcm', dispatch, xr)
        E = w1.shape[0]
        di = dispatched.reshape(E, -1, m)
        h = jax.nn.relu(jnp.einsum('ecm,emh->ech', di, w1))
        eo = jnp.einsum('ech,ehm->ecm', h, w2)
        eo = eo[None]
        out = jnp.einsum('szfc,zfcm->sm', combine, eo)
        return out.reshape(s, b, m)

    def _gn(v, G=32, eps=1e-05):
        B_, H_, W_, C_ = v.shape
        g = v.reshape(B_, H_, W_, G, C_ // G)
        m = jnp.mean(g, axis=(1, 2, 4), keepdims=True)
        s = jnp.var(g, axis=(1, 2, 4), keepdims=True)
        return ((g - m) / jnp.sqrt(s + eps)).reshape(v.shape)

    def _ln_c(v, eps=1e-06):
        m = jnp.mean(v, axis=-1, keepdims=True)
        s = jnp.var(v, axis=-1, keepdims=True)
        return (v - m) / jnp.sqrt(s + eps)

    def _ln_t(v, eps=1e-05):
        m = jnp.mean(v, axis=-1, keepdims=True)
        s = jnp.var(v, axis=-1, keepdims=True)
        return (v - m) / jnp.sqrt(s + eps)

    def _to_tokens(v):
        B_, H_, W_, C_ = v.shape
        return v.reshape(B_, H_ * W_, C_)

    def _from_tokens(t, like):
        return t.reshape(like.shape)
    x = x + _L0_conv_ref(_ln_c(x), L0_conv_Wq, L0_conv_bq, L0_conv_Wk, L0_conv_bk, L0_conv_Wv, L0_conv_bv, L0_conv_Wo, L0_conv_bo, L0_conv_sigma)
    t = _to_tokens(x)
    t = t + _L0_ffn_ref(_ln_t(t), L0_ffn_wg, L0_ffn_w1, L0_ffn_w2)
    x = _from_tokens(t, x)
    return x

_drawn_inputs = setup_inputs


def setup_inputs(seed=0):
    import zlib

    import numpy as np

    out = dict(_drawn_inputs(seed))
    spreads = {'L0_conv_bq': (0.0, 0.295),
     'L0_conv_bk': (0.0, 0.8),
     'L0_conv_bv': (0.0, 0.1),
     'L0_conv_bo': (0.0, 0.1)}
    factors = {}
    for name, (base, spread) in spreads.items():
        noise = np.random.default_rng([zlib.crc32(name.encode()), seed]).standard_normal(out[name].shape)
        drawn = base * np.exp(spread * noise) if base else spread * noise
        out[name] = jnp.asarray(drawn.astype(out[name].dtype))
    for name, factor in factors.items():
        out[name] = (out[name] * factor).astype(out[name].dtype)
    return out
```

```python
import numpy as np
from contextlib import ExitStack

import concourse.bass as bass
from concourse import mybir

B, HH, WW, D = 8, 16, 16, 256
TB = HH * WW
N = B * TB
P = 128
DC = D // P
NT = N // P
E, F = 8, 1024
CAP = N // E
FC = F // P
EPS_C, EPS_T = 1e-6, 1e-5
COL_TOK, COL_GATE, COL_NMR, COL_RSTD = D, D + 1, D + 2, D + 3
RW = D + 4
NOWHERE = 2 * N
OFF = -1e30


def shape_constants():
    p = np.arange(P)
    k = np.arange(P)
    same_row = (p[:, None] // WW) == (k[None, :] // WW)
    dist_row = np.where(same_row, (p[:, None] % WW - k[None, :] % WW) ** 2, 0).astype(np.float32)
    off_row = np.where(same_row, 0.0, OFF).astype(np.float32)
    kk = np.arange(TB)
    dist_col, off_col = [], []
    for t in range(TB // P):
        q = t * P + p
        same_col = (q[:, None] % WW) == (kk[None, :] % WW)
        dist_col.append(np.where(same_col, (q[:, None] // WW - kk[None, :] // WW) ** 2, 0))
        off_col.append(np.where(same_col, 0.0, OFF))
    dist_col = np.concatenate(dist_col, 1).astype(np.float32)
    off_col = np.concatenate(off_col, 1).astype(np.float32)
    ident = np.eye(P, dtype=np.float32)
    upper = (k[:, None] <= k[None, :]).astype(np.float32)
    rank = np.tile(E - np.arange(E), (P, 2)).astype(np.float32)
    f = np.concatenate([ident, upper, dist_row, off_row, dist_col, off_col, rank], 1)
    token = (np.arange(NT)[None, :] * P + p[:, None]).astype(np.int32)
    return np.ascontiguousarray(f), np.ascontiguousarray(token)


CONST_W = 4 * P + 4 * TB + 2 * E


def wait_apart(eng, sem, value, passed):
    wait(eng, sem, value)
    eng.sem_inc(passed, 1)


def wait(eng, sem, value):
    if isinstance(value, int) and value <= 0:
        return
    eng.wait_ge(sem, value)


class Chain:

    def __init__(self, eng, sem, start, steps):
        self.eng, self.sem, self.start, self.steps, self.n = eng, sem, start, steps, 0

    def mark(self, instruction):
        instruction.then_inc(self.sem, 1)
        self.n += 1

    def done(self, instruction=None):
        if instruction is not None:
            self.mark(instruction)
        self.eng.wait_ge(self.sem, self.start + self.n)

    def close(self):
        assert self.n == self.steps, (self.n, self.steps)


def build(nc, x, Wq, bq, Wk, bk, Wv, bv, Wo, bo, sigma, wg, w1, w2, consts, tokens, slots, out):
    f32, bf16, i32, u32 = mybir.dt.float32, mybir.dt.bfloat16, mybir.dt.int32, mybir.dt.uint32
    ALU, ACT, AX = mybir.AluOpType, mybir.ActivationFunctionType, mybir.AxisListType

    ctx = ExitStack()
    with ctx:
        def sb(name, shape, dt=f32):
            return ctx.enter_context(nc.sbuf_tensor(name, shape, dt))

        def bank(name):
            return ctx.enter_context(nc.psum_tensor(name, [P, 512], f32))

        def sem(name):
            return ctx.enter_context(nc.semaphore(name))

        const = sb("const", [P, CONST_W])
        ident = const[:, 0:P]
        upper_f = const[:, P:2 * P]
        dist_row, off_row = const[:, 2 * P:3 * P], const[:, 3 * P:4 * P]
        c0 = 4 * P
        dist_col, off_col = const[:, c0:c0 + 2 * TB], const[:, c0 + 2 * TB:c0 + 4 * TB]
        rank = const[:, c0 + 4 * TB:c0 + 4 * TB + 2 * E]
        token = sb("token", [P, NT], i32)
        upper = sb("upper", [P, P], bf16)
        ones = sb("ones", [P, P], bf16)
        wq_sb, wk_sb, wv_sb, wo_sb = (sb(n, [P, DC, D]) for n in ("wq_sb", "wk_sb", "wv_sb", "wo_sb"))
        bq_sb, bv_sb = sb("bq_sb", [P, DC]), sb("bv_sb", [P, DC])
        bv_wide = sb("bv_wide", [P, DC, P])
        bo_sb = sb("bo_sb", [P, D])
        wg_sb = sb("wg_sb", [P, DC, E])
        sigma_sb = sb("sigma_sb", [P, 1])
        decay = sb("decay", [P, 2])
        mask_row, mask_col = sb("mask_row", [P, P]), sb("mask_col", [P, 2 * TB])
        a_sb = sb("a_sb", [P, DC, D])
        woT = sb("woT", [P, DC, D])
        mT = sb("mT", [P, DC, D])
        qbias = sb("qbias", [P, DC])
        obias = sb("obias", [P, D])
        minus_half = sb("minus_half", [P, NT])
        x_sb = sb("x_sb", [P, NT, D])
        stats = sb("stats", [P, NT, 6])
        mean_var = sb("mean_var", [P, NT, 2])
        var_eps, rstd, nmr = sb("var_eps", [P, NT]), sb("rstd", [P, NT]), sb("nmr", [P, NT])
        xn = sb("xn", [P, 2, D])
        xb = [sb(f"xb{j}", [P, 2, D]) for j in range(2)]
        xT = [sb(f"xT{j}", [P, DC, TB]) for j in range(2)]
        qT = [sb(f"qT{j}", [P, DC, TB]) for j in range(2)]
        v_sb = sb("v_sb", [P, 2, D])
        s_row, s_col = sb("s_row", [P, 2, P]), sb("s_col", [P, 2, TB])
        top, ntop = sb("top", [P, 4]), sb("ntop", [P, 4])
        e_row, e_col = sb("e_row", [P, 2, P]), sb("e_col", [P, 2, TB])
        esum, einv = sb("esum", [P, 4]), sb("einv", [P, 4])
        prob = sb("prob", [P, 2, TB])
        pT = sb("pT", [P, 2, TB])
        row = [sb(f"row{j}", [P, 2, RW]) for j in range(2)]
        stats2, mean_var2 = sb("stats2", [P, 2, 6]), sb("mean_var2", [P, 2, 2])
        var_eps2 = sb("var_eps2", [P, 2])
        xn2 = sb("xn2", [P, 2, D])
        x2T = sb("x2T", [P, DC, TB])
        lmax, shifted, lexp = sb("lmax", [P, 2]), sb("shifted", [P, 2, E]), sb("lexp", [P, 2, E])
        ranked, rmax = sb("ranked", [P, 2, E]), sb("rmax", [P, 2])
        chosen = sb("chosen", [P, 2, E], bf16)
        both = sb("both", [P, E], bf16)
        before = [sb(f"before{j}", [P, E], bf16) for j in range(2)]
        gsum = sb("gsum", [P, 2])
        counted, loc, over, place = sb("counted", [P, 2, E]), sb("loc", [P, 2]), sb("over", [P, 2]), sb("place", [P, 2])
        slot = [sb(f"slot{j}", [P, 2], i32) for j in range(2)]
        empty = sb("empty", [P, RW])
        sl = sb("sl", [P, NT, RW])
        xs = [sb(f"xs{j}", [P, 2, D]) for j in range(2)]
        xgT = [sb(f"xgT{j}", [P, DC, CAP]) for j in range(2)]
        w1_sb = [sb(f"w1_sb{j}", [P, DC, F]) for j in range(2)]
        w2_sb = [sb(f"w2_sb{j}", [P, FC, D]) for j in range(2)]
        hT = [sb(f"hT{j}", [P, FC, CAP]) for j in range(2)]
        y = [sb(f"y{j}", [P, 2, D]) for j in range(2)]
        goal = [sb(f"goal{j}", [P, 2], i32) for j in range(2)]

        banks = [bank(f"bank{j}") for j in range(8)]

        def halves(j):
            return banks[j][:, :].rearrange("p (a b) -> p a b", a=2)

        ps_xT, ps_q, ps_s, ps_v, ps_pT, ps_o, ps_x2T = (halves(j) for j in range(7))
        ps_logit = banks[7][:, 0:2 * E].rearrange("p (a b) -> p a b", a=2)
        ps_count = banks[7][:, 2 * E:4 * E].rearrange("p (a b) -> p a b", a=2)
        ps_h = [halves(0), halves(1)]
        ps_gT = halves(6)
        ps_y = [halves(4), halves(5)]

        const_in, weights_in, small_in = sem("const_in"), sem("weights_in"), sem("small_in")
        x_in = [sem(f"x_in{j}") for j in range(4)]
        w1_in = [sem(f"w1_in{j}") for j in range(2)]
        w2_in = [sem(f"w2_in{j}") for j in range(2)]
        slots_in = [sem(f"slots_in{j}") for j in range(2)]
        x2_stored = [sem(f"x2_stored{j}") for j in range(2)]
        row_sent = [sem(f"row_sent{j}") for j in range(2)]
        y_sent = [sem(f"y_sent{j}") for j in range(2)]
        slots_empty, empty_ready = sem("slots_empty"), sem("empty_ready")
        tables = sem("tables")
        setup_step = sem("setup_step")
        fold_a, fold_wo, fold_m, fold_b = sem("fold_a"), sem("fold_wo"), sem("fold_m"), sem("fold_b")
        a_ready, wo_ready, m_ready, b_ready = sem("a_ready"), sem("wo_ready"), sem("m_ready"), sem("b_ready")
        var_ready, rstd_ready, nmr_ready = sem("var_ready"), sem("rstd_ready"), sem("nmr_ready")
        xn_ready, xb_ready = sem("xn_ready"), sem("xb_ready")
        xT_made, xT_ready = sem("xT_made"), sem("xT_ready")
        q_made, q_ready = sem("q_made"), sem("q_ready")
        s_made, top_ready = sem("s_made"), sem("top_ready")
        v_made, v_ready = sem("v_made"), sem("v_ready")
        e_ready, prob_ready = sem("e_ready"), sem("prob_ready")
        pT_made, pT_ready = sem("pT_made"), sem("pT_ready")
        o_made, x2_ready = sem("o_made"), sem("x2_ready")
        var2_ready, rstd2_ready, xn2_ready = sem("var2_ready"), sem("rstd2_ready"), sem("xn2_ready")
        x2T_made, x2T_ready = sem("x2T_made"), sem("x2T_ready")
        logit_made, shifted_ready, lexp_ready = sem("logit_made"), sem("shifted_ready"), sem("lexp_ready")
        chosen_ready, count_made, slot_ready = sem("chosen_ready"), sem("count_made"), sem("slot_ready")
        token_ready = sem("token_ready")
        attn_step, norm_step = sem("attn_step"), sem("norm_step")
        choose_step, place_step = sem("choose_step"), sem("place_step")
        xs_ready, gT_made, gT_ready = sem("xs_ready"), sem("gT_made"), sem("gT_ready")
        h_made, h_ready = sem("h_made"), sem("h_ready")
        y_made, y_ready = sem("y_made"), [sem(f"y_ready{j}") for j in range(2)]
        goal_ready = sem("goal_ready")

        pool_passed, dve_passed = sem("pool_passed"), sem("dve_passed")
        block = ctx.enter_context(nc.Block())
        x_view = x.rearrange("b h w d -> (b h w) d").rearrange("(t p) d -> p t d", p=P)
        out_rows = out.rearrange("b h w d -> (b h w) d")
        out_view = out_rows.rearrange("(t p) d -> p t d", p=P)
        slots_view = slots.rearrange("(t p) r -> p t r", p=P)
        w1_view = w1.rearrange("e (c p) f -> e p c f", p=P)
        w2_view = w2.rearrange("e (c p) d -> e p c d", p=P)

        def matrix(w):
            return w.rearrange("(c p) d -> p c d", p=P)

        def pairs(eng, first, last, body):
            assert (last - first) % 2 == 1
            with eng.Fori(0, (last - first + 1) // 2) as turn:
                for step in range(2):
                    n = first + step
                    body(turn + n // 2, n % 2)

        def peeled(n, body, **how):
            body(n // 2, n % 2, **how)

        @block.sync
        def _(sp):
            for g in range(4):
                sp.dma_start(x_sb[:, 4 * g:4 * g + 4, :], x_view[:, 4 * g:4 * g + 4, :]).then_inc(x_in[g], 16)
            sp.wait_ge(empty_ready, 1)
            sp.dma_start(slots_view, empty[:, None, :].to_broadcast([P, NT, RW])).then_inc(slots_empty, 16)
            for e in range(2):
                sp.dma_start(w1_sb[e][:, :, :], w1_view[e]).then_inc(w1_in[e], 16)
                sp.dma_start(w2_sb[e][:, :, :], w2_view[e]).then_inc(w2_in[e], 16)

            def store_x2(k, j):
                sp.wait_ge(x2_ready, 2 * k + j + 1)
                sp.dma_start(out_view[:, bass.ds(4 * k + 2 * j, 2), :], row[j][:, :, 0:D]).then_inc(x2_stored[j], 16)

            pairs(sp, 0, B - 1, store_x2)
            for j in range(2):
                sp.wait_ge(row_sent[j], 32 * (B // 2))

            def load_slots(k, j):
                wait(sp, slots_in[j], 16 * k)
                sp.dma_start(sl[:, bass.ds(4 * k + 2 * j, 2), :], slots_view[:, bass.ds(4 * k + 2 * j, 2), :]).then_inc(slots_in[j], 16)

            peeled(0, load_slots)
            peeled(1, load_slots)
            pairs(sp, 2, E - 1, load_slots)

            def load_weights(k, j):
                sp.wait_ge(h_made, (FC // 2) * (2 * k + j - 1))
                sp.dma_start(w1_sb[j][:, :, :], w1_view[2 * k + j]).then_inc(w1_in[j], 16)
                sp.wait_ge(y_made, 2 * k + j - 1)
                sp.dma_start(w2_sb[j][:, :, :], w2_view[2 * k + j]).then_inc(w2_in[j], 16)

            pairs(sp, 2, E - 1, load_weights)
            for j in range(2):
                sp.wait_ge(y_sent[j], 32 * (E // 2))
                sp.wait_ge(x2_stored[j], 16 * (B // 2))

        @block.gpsimd
        def _(pool):
            nc.gpsimd.memset(empty[:, :], 0.0).then_inc(token_ready, 1)
            pool.wait_ge(token_ready, 1)
            nc.gpsimd.memset(empty[:, COL_TOK:COL_TOK + 1].bitcast(i32), NOWHERE).then_inc(empty_ready, 1)
            for g, (a, b) in enumerate(((0, 4), (4, NT))):
                pool.wait_ge(var_ready, g + 1)
                nc.gpsimd.tensor_tensor(rstd[:, a:b], var_eps[:, a:b], minus_half[:, a:b], ALU.pow).then_inc(rstd_ready, 1)
            pool.wait_ge(b_ready, 1)
            pool.wait_ge(slots_empty, 16)

            def scatter_rows(k, j):
                wait_apart(pool, slot_ready, 2 * k + j + 1, pool_passed)
                for t in range(2):
                    nc.gpsimd.indirect_dma_start(
                        slots, bass.IndirectOffsetOnAxis(ap=slot[j][:, t:t + 1].bitcast(u32), axis=0),
                        row[j][:, t, :], None, bounds_check=N - 1, oob_is_err=False).then_inc(row_sent[j], 16)

            def batch(k, j, before_it=True):
                i = 2 * k + j
                wait(pool, x2_ready, i - 1)
                nc.gpsimd.tensor_tensor(xb[j][:, :, :], x_sb[:, bass.ds(4 * k + 2 * j, 2), :],
                                        obias[:, None, :].to_broadcast([P, 2, D]), ALU.add).then_inc(xb_ready, 1)
                if before_it:
                    if j == 1:
                        scatter_rows(k, 0)
                    else:
                        scatter_rows(k - 1, 1)
                pool.wait_ge(var2_ready, i + 1)
                nc.gpsimd.tensor_tensor(row[j][:, :, COL_RSTD], var_eps2[:, :], minus_half[:, 0:2], ALU.pow).then_inc(rstd2_ready, 1)

            peeled(0, batch, before_it=False)
            pairs(pool, 1, B - 2, batch)
            peeled(B - 1, batch)
            scatter_rows(B // 2 - 1, 1)

            for j in range(2):
                pool.wait_ge(x2_stored[j], 16 * (B // 2))

            def scatter_y(k, j):
                wait_apart(pool, y_ready[j], k + 1, pool_passed)
                for c in range(2):
                    nc.gpsimd.indirect_dma_start(
                        out_rows, bass.IndirectOffsetOnAxis(ap=goal[j][:, c:c + 1].bitcast(u32), axis=0),
                        y[j][:, c, :], None, bounds_check=N - 1, oob_is_err=False).then_inc(y_sent[j], 16)

            pairs(pool, 0, E - 1, scatter_y)

        @block.tensor
        def _(pe):
            pe.wait_ge(weights_in, 64)
            for d in range(DC):
                for c in range(DC):
                    step = nc.tensor.matmul(ps_q[:, d, :], wq_sb[:, c, d * P:(d + 1) * P], wk_sb[:, c, :], start=c == 0, stop=c == DC - 1)
            step.then_inc(fold_a, 1)
            pe.wait_ge(const_in, 32)
            for c in range(DC):
                for m in range(DC):
                    step = nc.tensor.transpose(ps_s[:, m, c * P:(c + 1) * P], wo_sb[:, c, m * P:(m + 1) * P], ident)
            step.then_inc(fold_wo, 1)
            pe.wait_ge(small_in, 80)
            pe.wait_ge(tables, 1)
            for d in range(DC):
                for c in range(DC):
                    step = nc.tensor.matmul(banks[7][:, 4 * E + d:4 * E + d + 1], wk_sb[:, c, d * P:(d + 1) * P], bq_sb[:, c:c + 1], start=c == 0, stop=c == DC - 1)
            step.then_inc(fold_b, 1)

            def transpose_x(k, j):
                i = 2 * k + j
                pe.wait_ge(xn_ready, i + 1)
                wait(pe, xT_ready, i)
                for t in range(2):
                    for c in range(DC):
                        step = nc.tensor.transpose(ps_xT[:, c, t * P:(t + 1) * P], xn[:, t, c * P:(c + 1) * P], ident)
                step.then_inc(xT_made, 1)

            def query(k, j):
                i = 2 * k + j
                pe.wait_ge(xT_ready, i + 1)
                wait(pe, q_ready, 2 * i)
                for d in range(DC):
                    for c in range(DC):
                        step = nc.tensor.matmul(ps_q[:, d, :], a_sb[:, c, d * P:(d + 1) * P], xT[j][:, c, :], start=c == 0, stop=c == DC - 1)
                step.then_inc(q_made, 1)

            def batch(k, j, before_it=True, next_one=True):
                i = 2 * k + j
                kn, jn = (k, 1) if j == 0 else (k + 1, 0)
                pe.wait_ge(q_ready, 2 * i + 2)
                wait(pe, top_ready, i)
                for t in range(2):
                    for c in range(DC):
                        step = nc.tensor.matmul(ps_s[:, t, :], qT[j][:, c, t * P:(t + 1) * P], xT[j][:, c, :], start=c == 0, stop=c == DC - 1)
                step.then_inc(s_made, 1)
                wait(pe, v_ready, i)
                for t in range(2):
                    for c in range(DC):
                        step = nc.tensor.matmul(ps_v[:, t, :], xT[j][:, c, t * P:(t + 1) * P], mT[:, c, :], start=c == 0, stop=c == DC - 1)
                step.then_inc(v_made, 1)
                if next_one:
                    transpose_x(kn, jn)
                if before_it:
                    transpose_x2(i - 1)
                if next_one:
                    query(kn, jn)
                pe.wait_ge(prob_ready, i + 1)
                wait(pe, pT_ready, i)
                for t in range(2):
                    for c in range(2):
                        step = nc.tensor.transpose(ps_pT[:, c, t * P:(t + 1) * P], prob[:, t, c * P:(c + 1) * P], ident)
                step.then_inc(pT_made, 1)
                if before_it:
                    logits(i - 1)
                pe.wait_ge(pT_ready, i + 1)
                pe.wait_ge(v_ready, i + 1)
                wait(pe, x2_ready, i)
                for t in range(2):
                    for c in range(2):
                        step = nc.tensor.matmul(ps_o[:, t, :], pT[:, c, t * P:(t + 1) * P], v_sb[:, c, :], start=c == 0, stop=c == 1)
                step.then_inc(o_made, 1)
                if before_it:
                    counts(i - 1, 1 - j)

            def transpose_x2(i):
                pe.wait_ge(xn2_ready, i + 1)
                wait(pe, x2T_ready, i)
                for t in range(2):
                    for c in range(DC):
                        step = nc.tensor.transpose(ps_x2T[:, c, t * P:(t + 1) * P], xn2[:, t, c * P:(c + 1) * P], ident)
                step.then_inc(x2T_made, 1)

            def logits(i):
                pe.wait_ge(x2T_ready, i + 1)
                wait(pe, slot_ready, i)
                for t in range(2):
                    for c in range(DC):
                        step = nc.tensor.matmul(ps_logit[:, t, :], x2T[:, c, t * P:(t + 1) * P], wg_sb[:, c, :], start=c == 0, stop=c == DC - 1)
                step.then_inc(logit_made, 1)

            def counts(i, j):
                pe.wait_ge(chosen_ready, i + 1)
                nc.tensor.matmul(ps_count[:, 0, :], upper[:, :], chosen[:, 0, :], start=True, stop=False)
                nc.tensor.matmul(ps_count[:, 0, :], ones[:, :], before[j][:, :], start=False, stop=True)
                nc.tensor.matmul(ps_count[:, 1, :], upper[:, :], chosen[:, 1, :], start=True, stop=False)
                nc.tensor.matmul(ps_count[:, 1, :], ones[:, :], chosen[:, 0, :], start=False, stop=False)
                nc.tensor.matmul(ps_count[:, 1, :], ones[:, :], before[j][:, :], start=False, stop=True).then_inc(count_made, 1)

            peeled(0, transpose_x)
            pe.wait_ge(wo_ready, 1)
            for d in range(DC):
                for m in range(DC):
                    step = nc.tensor.matmul(ps_v[:, d, :], wv_sb[:, m, d * P:(d + 1) * P], woT[:, m, :], start=m == 0, stop=m == DC - 1)
            step.then_inc(fold_m, 1)
            for m in range(DC):
                step = nc.tensor.matmul(banks[5][:, 0:D], bv_wide[:, m, :], woT[:, m, :], start=m == 0, stop=m == DC - 1)
            step.then_inc(fold_b, 1)
            pe.wait_ge(a_ready, 1)
            peeled(0, query)
            pe.wait_ge(m_ready, 1)
            pe.wait_ge(b_ready, 1)
            peeled(0, batch, before_it=False)
            pairs(pe, 1, B - 2, batch)
            peeled(B - 1, batch, next_one=False)
            transpose_x2(B - 1)
            logits(B - 1)
            counts(B - 1, (B - 1) % 2)

            def gather_T(k, j):
                e = 2 * k + j
                pe.wait_ge(xs_ready, e + 1)
                wait(pe, gT_ready, e)
                for t in range(2):
                    for c in range(DC):
                        step = nc.tensor.transpose(ps_gT[:, c, t * P:(t + 1) * P], xs[j][:, t, c * P:(c + 1) * P], ident)
                step.then_inc(gT_made, 1)

            def hidden(k, j):
                e = 2 * k + j
                pe.wait_ge(w1_in[j], 16 * (k + 1))
                pe.wait_ge(gT_ready, e + 1)
                for q in range(FC // 2):
                    wait(pe, h_ready, (FC // 2) * e + q - 1)
                    for u in range(2):
                        f = 2 * q + u
                        for c in range(DC):
                            step = nc.tensor.matmul(ps_h[q % 2][:, u, :], w1_sb[j][:, c, f * P:(f + 1) * P], xgT[j][:, c, :], start=c == 0, stop=c == DC - 1)
                    step.then_inc(h_made, 1)

            def expert_out(k, j):
                e = 2 * k + j
                pe.wait_ge(w2_in[j], 16 * (k + 1))
                pe.wait_ge(h_ready, (FC // 2) * (e + 1))
                wait(pe, y_ready[j], k)
                for t in range(2):
                    for f in range(FC):
                        step = nc.tensor.matmul(ps_y[j][:, t, :], hT[j][:, f, t * P:(t + 1) * P], w2_sb[j][:, f, :], start=f == 0, stop=f == FC - 1)
                step.then_inc(y_made, 1)

            def expert(k, j, two_on=True):
                hidden(*((k, 1) if j == 0 else (k + 1, 0)))
                if two_on:
                    gather_T(k + 1, j)
                expert_out(k, j)

            peeled(0, gather_T)
            peeled(1, gather_T)
            peeled(0, hidden)
            pairs(pe, 0, E - 3, expert)
            peeled(E - 2, expert, two_on=False)
            peeled(E - 1, expert_out)

        @block.scalar
        def _(act):
            for dst, src in ((wq_sb, Wq), (wk_sb, Wk), (wo_sb, Wo), (wv_sb, Wv)):
                act.dma_start(dst[:, :, :], matrix(src)).then_inc(weights_in, 16)
            act.dma_start(const[:, :], consts).then_inc(const_in, 16)
            act.dma_start(token[:, :], tokens).then_inc(const_in, 16)
            with nc.allow_non_contiguous_dma(reason="bias columns of 128"):
                act.dma_start(bq_sb[:, :], bq.rearrange("(c p) -> p c", p=P)).then_inc(small_in, 16)
                act.dma_start(bv_sb[:, :], bv.rearrange("(c p) -> p c", p=P)).then_inc(small_in, 16)
            act.dma_start(sigma_sb[:, :], sigma[None, :].to_broadcast([P, 1])).then_inc(small_in, 16)
            act.dma_start(bo_sb[:, :], bo[None, :].to_broadcast([P, D])).then_inc(small_in, 16)
            act.dma_start(wg_sb[:, :, :], wg.rearrange("(c p) e -> p c e", p=P)).then_inc(small_in, 16)

            act.wait_ge(fold_a, 1)
            nc.scalar.activation(a_sb[:, :, :], ps_q, ACT.Copy).then_inc(a_ready, 1)
            act.wait_ge(fold_wo, 1)
            nc.scalar.activation(woT[:, :, :], ps_s, ACT.Copy).then_inc(wo_ready, 1)
            act.wait_ge(fold_m, 1)
            nc.scalar.activation(mT[:, :, :], ps_v, ACT.Copy).then_inc(m_ready, 1)
            act.wait_ge(b_ready, 1)

            def query(k, j):
                i = 2 * k + j
                act.wait_ge(q_made, i + 1)
                for d in range(DC):
                    nc.scalar.activation(qT[j][:, d, :], ps_q[:, d, :], ACT.Identity, bias=qbias[:, d:d + 1]).then_inc(q_ready, 1)

            def batch(k, j, before_it=True, next_one=True):
                i = 2 * k + j
                act.wait_ge(top_ready, i + 1)
                for t in range(2):
                    nc.scalar.activation(e_col[:, t, :], s_col[:, t, :], ACT.Exp, bias=ntop[:, t:t + 1], accum_out=esum[:, t:t + 1]).then_inc(e_ready, 1)
                    nc.scalar.activation(e_row[:, t, :], s_row[:, t, :], ACT.Exp, bias=ntop[:, 2 + t:3 + t], accum_out=esum[:, 2 + t:3 + t]).then_inc(e_ready, 1)
                if before_it:
                    transposed_x2(i - 1)
                act.wait_ge(v_made, i + 1)
                wait(act, o_made, i)
                nc.scalar.activation(v_sb[:, :, :], ps_v, ACT.Copy).then_inc(v_ready, 1)
                if next_one:
                    query(*((k, 1) if j == 0 else (k + 1, 0)))
                act.wait_ge(pT_made, i + 1)
                nc.scalar.activation(pT[:, :, :], ps_pT, ACT.Copy).then_inc(pT_ready, 1)
                if before_it:
                    gate_exp(i - 1)

            def transposed_x2(i):
                act.wait_ge(x2T_made, i + 1)
                wait(act, logit_made, i)
                nc.scalar.activation(x2T[:, :, :], ps_x2T, ACT.Copy).then_inc(x2T_ready, 1)

            def gate_exp(i):
                act.wait_ge(shifted_ready, i + 1)
                nc.scalar.activation(lexp[:, :, :], shifted[:, :, :], ACT.Exp).then_inc(lexp_ready, 1)

            peeled(0, query)
            peeled(0, batch, before_it=False)
            pairs(act, 1, B - 2, batch)
            peeled(B - 1, batch, next_one=False)
            transposed_x2(B - 1)
            gate_exp(B - 1)

            def gathered_T(k, j):
                act.wait_ge(gT_made, 2 * k + j + 1)
                wait(act, h_made, (FC // 2) * (2 * k + j - 1))
                nc.scalar.activation(xgT[j][:, :, :], ps_gT, ACT.Copy).then_inc(gT_ready, 1)

            def hidden(k, j):
                e = 2 * k + j
                wait(act, y_made, e - 1)
                for q in range(FC // 2):
                    act.wait_ge(h_made, (FC // 2) * e + q + 1)
                    nc.scalar.activation(hT[j][:, 2 * q:2 * q + 2, :], ps_h[q % 2], ACT.Relu).then_inc(h_ready, 1)

            def expert(k, j, two_on=True):
                hidden(*((k, 1) if j == 0 else (k + 1, 0)))
                if two_on:
                    gathered_T(k + 1, j)

            peeled(0, gathered_T)
            peeled(1, gathered_T)
            peeled(0, hidden)
            pairs(act, 0, E - 3, expert)
            peeled(E - 2, expert, two_on=False)

        @block.vector
        def _(dve):
            setup = Chain(dve, setup_step, 0, None)
            nc.vector.memset(minus_half[:, :], -0.5)
            nc.vector.memset(before[0][:, :], 0.0)
            setup.mark(nc.vector.memset(ones[:, :], 1.0))
            setup.done(nc.vector.memset(bv_wide[:, :, :], 1.0))

            def first_norm(a, b):
                for i in range(a, b):
                    if i % 4 == 0:
                        dve.wait_ge(x_in[i // 4], 16)
                    setup.mark(nc.vector.bn_stats(stats[:, i, :], x_sb[:, i, :]))
                setup.done()
                for i in range(a, b):
                    setup.mark(nc.vector.bn_aggr(mean_var[:, i, :], stats[:, i, :]))
                setup.done()
                nc.vector.tensor_scalar(var_eps[:, a:b], mean_var[:, a:b, 1], EPS_C, None, ALU.add).then_inc(var_ready, 1)

            def first_norm_offsets(g, a, b):
                dve.wait_ge(rstd_ready, g + 1)
                nc.vector.scalar_tensor_tensor(nmr[:, a:b], mean_var[:, a:b, 0], -1.0, rstd[:, a:b], ALU.mult, ALU.mult).then_inc(nmr_ready, 1)

            first_norm(0, 4)
            dve.wait_ge(small_in, 80)
            for c in range(DC):
                setup.mark(nc.vector.tensor_scalar(bv_wide[:, c, :], bv_wide[:, c, :], bv_sb[:, c:c + 1], None, ALU.mult))
            dve.wait_ge(const_in, 32)
            nc.vector.tensor_copy(upper[:, :], upper_f).then_inc(tables, 1)
            setup.done(nc.vector.tensor_tensor(decay[:, 0:1], sigma_sb[:, :], sigma_sb[:, :], ALU.mult))
            setup.done(nc.vector.reciprocal(decay[:, 1:2], decay[:, 0:1]))
            setup.done(nc.vector.tensor_scalar(decay[:, 0:1], decay[:, 1:2], -0.5, None, ALU.mult))
            setup.mark(nc.vector.scalar_tensor_tensor(mask_row[:, :], dist_row, decay[:, 0:1], off_row, ALU.mult, ALU.add))
            setup.mark(nc.vector.scalar_tensor_tensor(mask_col[:, :], dist_col, decay[:, 0:1], off_col, ALU.mult, ALU.add))
            first_norm_offsets(0, 0, 4)
            dve.wait_ge(fold_b, 1)
            setup.mark(nc.vector.tensor_copy(qbias[:, :], banks[7][:, 4 * E:4 * E + DC]))

            def normalised_x(k, j):
                i = 2 * k + j
                wait(dve, xT_made, i)
                for t in range(2):
                    r = 4 * k + 2 * j + t
                    step = nc.vector.tensor_scalar(xn[:, t, :], x_sb[:, bass.ds(r, 1), :], rstd[:, bass.ds(r, 1)],
                                                   nmr[:, bass.ds(r, 1)], ALU.mult, ALU.add)
                step.then_inc(xn_ready, 1)

            def transposed_x(k, j):
                i = 2 * k + j
                dve.wait_ge(xT_made, i + 1)
                wait(dve, v_made, i - 1)
                wait(dve, s_made, i - 1)
                nc.vector.tensor_copy(xT[j][:, :, :], ps_xT).then_inc(xT_ready, 1)

            dve.wait_ge(nmr_ready, 1)
            peeled(0, normalised_x)
            peeled(0, transposed_x)
            dve.wait_ge(fold_b, 2)
            nc.vector.scalar_tensor_tensor(obias[:, :], banks[5][:, 0:D], 2.0, bo_sb[:, :], ALU.mult, ALU.add).then_inc(b_ready, 1)
            first_norm(4, NT)
            first_norm_offsets(1, 4, NT)
            dve.wait_ge(nmr_ready, 2)

            def maxima(k, j):
                i = 2 * k + j
                chain = Chain(dve, attn_step, 8 * i, 5)
                wait_apart(dve, s_made, i + 1, dve_passed)
                for t in range(2):
                    chain.mark(nc.vector.tensor_tensor_reduce(
                        out=s_col[:, t, :], in0=ps_s[:, t, :], in1=mask_col[:, t * TB:(t + 1) * TB], scale=1.0,
                        scalar=-3e38, op0=ALU.add, op1=ALU.max, accum_out=top[:, t:t + 1]))
                    chain.mark(nc.vector.tensor_tensor_reduce(
                        out=s_row[:, t, :], in0=ps_s[:, t, t * P:(t + 1) * P], in1=mask_row[:, :], scale=1.0,
                        scalar=-3e38, op0=ALU.add, op1=ALU.max, accum_out=top[:, 2 + t:3 + t]))
                chain.done()
                nc.vector.tensor_scalar(ntop[:, :], top[:, :], -1.0, None, ALU.mult).then_inc(top_ready, 1)

            def probabilities(k, j):
                i = 2 * k + j
                chain = Chain(dve, attn_step, 8 * i + 4, 3)
                dve.wait_ge(e_ready, 4 * i + 4)
                chain.done(nc.vector.reciprocal(einv[:, :], esum[:, :]))
                wait(dve, pT_made, i)
                for t in range(2):
                    chain.mark(nc.vector.tensor_scalar(prob[:, t, :], e_col[:, t, :], einv[:, t:t + 1], None, ALU.mult))
                chain.done()
                own = [prob[:, t, t * P:(t + 1) * P] for t in range(2)]
                nc.vector.scalar_tensor_tensor(own[0], e_row[:, 0, :], einv[:, 2:3], own[0], ALU.mult, ALU.add).then_inc(attn_step, 1)
                nc.vector.scalar_tensor_tensor(own[1], e_row[:, 1, :], einv[:, 3:4], own[1], ALU.mult, ALU.add).then_inc(prob_ready, 1)

            def residual(k, j):
                i = 2 * k + j
                chain = Chain(dve, norm_step, 5 * i, 4)
                dve.wait_ge(o_made, i + 1)
                dve.wait_ge(xb_ready, i + 1)
                wait(dve, x2_stored[j], 16 * k)
                wait(dve, row_sent[j], 32 * k)
                nc.vector.tensor_tensor(row[j][:, :, 0:D], ps_o, xb[j][:, :, :], ALU.add).then_inc(x2_ready, 1)
                dve.wait_ge(x2_ready, i + 1)
                for t in range(2):
                    chain.mark(nc.vector.bn_stats(stats2[:, t, :], row[j][:, t, 0:D]))
                chain.done()
                dve.sem_inc(dve_passed, 1)
                for t in range(2):
                    chain.mark(nc.vector.bn_aggr(mean_var2[:, t, :], stats2[:, t, :]))
                chain.done()
                nc.vector.tensor_scalar(var_eps2[:, :], mean_var2[:, :, 1], EPS_T, None, ALU.add).then_inc(var2_ready, 1)

            def normalised(k, j):
                i = 2 * k + j
                chain = Chain(dve, norm_step, 5 * i + 4, 1)
                dve.wait_ge(rstd2_ready, i + 1)
                chain.done(nc.vector.scalar_tensor_tensor(row[j][:, :, COL_NMR], mean_var2[:, :, 0], -1.0, row[j][:, :, COL_RSTD], ALU.mult, ALU.mult))
                wait(dve, x2T_made, i)
                for t in range(2):
                    step = nc.vector.tensor_scalar(xn2[:, t, :], row[j][:, t, 0:D], row[j][:, t, COL_RSTD:COL_RSTD + 1],
                                                   row[j][:, t, COL_NMR:COL_NMR + 1], ALU.mult, ALU.add)
                step.then_inc(xn2_ready, 1)

            def wide(a):
                return a.unsqueeze(2).to_broadcast([P, 2, E])

            def choose(k, j):
                i = 2 * k + j
                chain = Chain(dve, choose_step, 6 * i, 6)
                dve.wait_ge(logit_made, i + 1)
                chain.done(nc.vector.tensor_reduce(lmax[:, :], ps_logit, axis=AX.X, op=ALU.max))
                nc.vector.tensor_tensor(shifted[:, :, :], ps_logit, wide(lmax[:, :]), ALU.subtract).then_inc(shifted_ready, 1)
                dve.wait_ge(shifted_ready, i + 1)
                chain.done(nc.vector.scalar_tensor_tensor(ranked[:, :, :], shifted[:, :, :], 0.0, rank.rearrange("p (a b) -> p a b", a=2), ALU.is_equal, ALU.mult))
                chain.done(nc.vector.tensor_reduce(rmax[:, :], ranked[:, :, :], axis=AX.X, op=ALU.max))
                nc.vector.tensor_tensor(chosen[:, :, :], rank.rearrange("p (a b) -> p a b", a=2), wide(rmax[:, :]), ALU.is_equal).then_inc(chosen_ready, 1)
                wait(dve, count_made, i)
                dve.wait_ge(chosen_ready, i + 1)
                chain.done(nc.vector.tensor_tensor(both[:, :], chosen[:, 0, :], chosen[:, 1, :], ALU.add))
                chain.done(nc.vector.tensor_tensor(before[1 - j][:, :], before[j][:, :], both[:, :], ALU.add))
                chain.mark(nc.vector.tensor_copy(row[j][:, :, COL_TOK].bitcast(i32), token[:, bass.ds(4 * k + 2 * j, 2)]))
                chain.close()

            def place_rows(k, j):
                i = 2 * k + j
                chain = Chain(dve, place_step, 6 * i, 6)
                dve.wait_ge(lexp_ready, i + 1)
                chain.mark(nc.vector.tensor_reduce(gsum[:, :], lexp[:, :, :], axis=AX.X, op=ALU.add))
                dve.wait_ge(count_made, i + 1)
                chain.done(nc.vector.tensor_tensor(counted[:, :, :], ps_count, chosen[:, :, :], ALU.mult))
                chain.mark(nc.vector.reciprocal(row[j][:, :, COL_GATE], gsum[:, :]))
                chain.done(nc.vector.tensor_reduce(loc[:, :], counted[:, :, :], axis=AX.X, op=ALU.add))
                chain.mark(nc.vector.tensor_scalar(over[:, :], loc[:, :], float(CAP), float(NOWHERE), ALU.is_gt, ALU.mult))
                chain.done(nc.vector.scalar_tensor_tensor(place[:, :], rmax[:, :], -float(CAP), loc[:, :], ALU.mult, ALU.add))
                nc.vector.scalar_tensor_tensor(slot[j][:, :], place[:, :], float(CAP * E - 1), over[:, :], ALU.add, ALU.add).then_inc(slot_ready, 1)
                chain.close()

            def batch(k, j, before_it=True, next_one=True):
                kb, jb = (k, 0) if j == 1 else (k - 1, 1)
                if before_it:
                    residual(kb, jb)
                if next_one:
                    normalised_x(*((k, 1) if j == 0 else (k + 1, 0)))
                maxima(k, j)
                if before_it:
                    normalised(kb, jb)
                if next_one:
                    transposed_x(*((k, 1) if j == 0 else (k + 1, 0)))
                probabilities(k, j)
                if before_it:
                    choose(kb, jb)
                    place_rows(kb, jb)

            peeled(0, batch, before_it=False)
            pairs(dve, 1, B - 2, batch)
            peeled(B - 1, batch, next_one=False)
            for part in (residual, normalised, choose, place_rows):
                peeled(B - 1, part)

            def gathered(k, j):
                e = 2 * k + j
                dve.wait_ge(slots_in[j], 16 * (k + 1))
                wait(dve, gT_made, e - 1)
                for t in range(2):
                    r = 4 * k + 2 * j + t
                    step = nc.vector.tensor_scalar(xs[j][:, t, :], sl[:, bass.ds(r, 1), 0:D], sl[:, bass.ds(r, 1), COL_RSTD:COL_RSTD + 1],
                                                   sl[:, bass.ds(r, 1), COL_NMR:COL_NMR + 1], ALU.mult, ALU.add)
                step.then_inc(xs_ready, 1)

            def output_rows(k, j):
                e = 2 * k + j
                wait(dve, y_sent[j], 32 * k)
                nc.vector.tensor_copy(goal[j][:, :], sl[:, bass.ds(4 * k + 2 * j, 2), COL_TOK].bitcast(i32)).then_inc(goal_ready, 1)
                dve.wait_ge(y_made, e + 1)
                for t in range(2):
                    r = 4 * k + 2 * j + t
                    step = nc.vector.scalar_tensor_tensor(y[j][:, t, :], ps_y[j][:, t, :], sl[:, bass.ds(r, 1), COL_GATE:COL_GATE + 1],
                                                          sl[:, bass.ds(r, 1), 0:D], ALU.mult, ALU.add)
                step.then_inc(y_ready[j], 1)

            def expert(k, j, two_on=True):
                if two_on:
                    gathered(k + 1, j)
                output_rows(k, j)

            peeled(0, gathered)
            peeled(1, gathered)
            pairs(dve, 0, E - 3, expert)
            peeled(E - 2, expert, two_on=False)
            peeled(E - 1, expert, two_on=False)


_INS = ["x", "L0_conv_Wq", "L0_conv_bq", "L0_conv_Wk", "L0_conv_bk", "L0_conv_Wv", "L0_conv_bv", "L0_conv_Wo",
        "L0_conv_bo", "L0_conv_sigma", "L0_ffn_wg", "L0_ffn_w1", "L0_ffn_w2"]


def kernel(**inputs):
    import concourse.bacc as bacc
    from concourse.bass_utils import run_bass_kernel_spmd

    nc = bacc.Bacc("TRN2", target_bir_lowering=False, num_devices=1)
    arrays, args = {}, []
    table, token = shape_constants()
    for name, a in [(n, inputs[n]) for n in _INS] + [("consts", table), ("tokens", token)]:
        a = np.ascontiguousarray(a)
        arrays[f"in_{name}"] = a
        args.append(nc.dram_tensor(f"in_{name}", a.shape, mybir.dt.from_np(a.dtype), kind="ExternalInput").ap())
    slots = nc.dram_tensor("slots", [N, RW], mybir.dt.float32, kind="Internal").ap()
    out = nc.dram_tensor("out_0", [B, HH, WW, D], mybir.dt.float32, kind="ExternalOutput").ap()
    build(nc, *args, slots, out)
    r = run_bass_kernel_spmd(nc, [arrays], core_ids=[0])
    return r.results[0]["out_0"]
```

```python
import numpy as np
from contextlib import ExitStack

import concourse.bass as bass
from concourse import mybir

B, HH, WW, D = 8, 16, 16, 256
TB = HH * WW
N = B * TB
P = 128
DC = D // P
NT = N // P
E, F = 8, 1024
CAP = N // E
FC = F // P
EPS_C, EPS_T = 1e-6, 1e-5
COL_TOK, COL_GATE, COL_NMR, COL_RSTD = D, D + 1, D + 2, D + 3
RW = D + 4
NOWHERE = 2 * N
OFF = -1e30


def shape_constants():
    p = np.arange(P)
    k = np.arange(P)
    kk = np.arange(TB)
    same_row = (p[:, None] // WW) == (k[None, :] // WW)
    dist_row = np.where(same_row, (p[:, None] % WW - k[None, :] % WW) ** 2, 0)
    same_col = (p[:, None] % WW) == (kk[None, :] % WW)
    dist_col = [np.where(same_col, ((t * P + p[:, None]) // WW - kk[None, :] // WW) ** 2, 0) for t in range(TB // P)]
    upper = k[:, None] <= k[None, :]
    rank = np.tile(E - np.arange(E), (P, 2))
    table = np.concatenate([upper, dist_row, ~same_row, *dist_col, ~same_col, rank], 1).astype(np.float16)
    ident = np.eye(P, dtype=np.float32)
    token = (np.arange(NT)[None, :] * P + p[:, None]).astype(np.int32)
    return np.ascontiguousarray(table), ident, np.ascontiguousarray(token)


TABLE_W = 3 * P + 3 * TB + 2 * E


def wait_apart(eng, sem, value, passed):
    wait(eng, sem, value)
    eng.sem_inc(passed, 1)


def wait(eng, sem, value):
    if isinstance(value, int) and value <= 0:
        return
    eng.wait_ge(sem, value)


class Chain:

    def __init__(self, eng, sem, start, steps):
        self.eng, self.sem, self.start, self.steps, self.n = eng, sem, start, steps, 0

    def mark(self, instruction):
        instruction.then_inc(self.sem, 1)
        self.n += 1

    def done(self, instruction=None):
        if instruction is not None:
            self.mark(instruction)
        self.eng.wait_ge(self.sem, self.start + self.n)

    def close(self):
        assert self.n == self.steps, (self.n, self.steps)


def build(nc, x, Wq, bq, Wk, bk, Wv, bv, Wo, bo, sigma, wg, w1, w2, tables_in, eye, tokens, slots, out):
    f32, f32r, f16, bf16, i32, u32 = mybir.dt.float32, mybir.dt.float32r, mybir.dt.float16, mybir.dt.bfloat16, mybir.dt.int32, mybir.dt.uint32
    ALU, ACT, AX = mybir.AluOpType, mybir.ActivationFunctionType, mybir.AxisListType

    ctx = ExitStack()
    with ctx:
        def sb(name, shape, dt=f32):
            return ctx.enter_context(nc.sbuf_tensor(name, shape, dt))

        def bank(name):
            return ctx.enter_context(nc.psum_tensor(name, [P, 512], f32))

        def sem(name):
            return ctx.enter_context(nc.semaphore(name))

        table = sb("table", [P, TABLE_W], f16)
        upper_in, dist_row, far_row = (table[:, n * P:(n + 1) * P] for n in range(3))
        dist_col, far_col = table[:, 3 * P:3 * P + 2 * TB], table[:, 3 * P + 2 * TB:3 * P + 3 * TB]
        rank = table[:, 3 * P + 3 * TB:TABLE_W].rearrange("p (a b) -> p a b", a=2)
        ident_sb = sb("ident", [P, P])
        ident = ident_sb[:, :]
        token = sb("token", [P, NT], i32)
        upper = sb("upper", [P, P], bf16)
        ones = sb("ones", [P, P], bf16)
        w1_in_sb, w2_in_sb = sb("w1_in_sb", [P, DC, F]), sb("w2_in_sb", [P, FC, D])
        wq_sb, wk_sb, wv_sb, wo_sb = (w2_in_sb[:, DC * n:DC * (n + 1), :] for n in range(4))
        bq_sb, bv_sb = sb("bq_sb", [P, DC]), sb("bv_sb", [P, DC])
        bv_wide = sb("bv_wide", [P, DC, P])
        bo_sb = sb("bo_sb", [P, D])
        wg_sb = sb("wg_sb", [P, DC, E])
        sigma_sb = sb("sigma_sb", [P, 1])
        decay = sb("decay", [P, 2])
        mask_row, mask_col = sb("mask_row", [P, P]), sb("mask_col", [P, 2 * TB])
        a_sb = sb("a_sb", [P, DC, D])
        woT = sb("woT", [P, DC, D])
        mT = sb("mT", [P, DC, D])
        qbias = sb("qbias", [P, DC])
        obias = sb("obias", [P, D])
        minus_half = sb("minus_half", [P, NT])
        sl_sb = sb("sl", [P, NT * RW])
        sl = sl_sb[:, :].rearrange("p (t r) -> p t r", t=NT)
        x_sb = sl_sb[:, 0:NT * D].rearrange("p (t d) -> p t d", t=NT)
        stats = sb("stats", [P, NT, 6])
        mean_var = sb("mean_var", [P, NT, 2])
        var_eps, rstd, nmr = sb("var_eps", [P, NT]), sb("rstd", [P, NT]), sb("nmr", [P, NT])
        xn = sb("xn", [P, 2, D])
        xb = [sb(f"xb{j}", [P, 2, D]) for j in range(2)]
        xT = [sb(f"xT{j}", [P, DC, TB]) for j in range(2)]
        qT = [sb(f"qT{j}", [P, DC, TB]) for j in range(2)]
        v_sb = sb("v_sb", [P, 2, D])
        s_row, s_col = sb("s_row", [P, 2, P]), sb("s_col", [P, 2, TB])
        top, ntop = sb("top", [P, 4]), sb("ntop", [P, 4])
        e_row, e_col = sb("e_row", [P, 2, P]), sb("e_col", [P, 2, TB])
        esum, einv = sb("esum", [P, 4]), sb("einv", [P, 4])
        prob = sb("prob", [P, 2, TB])
        pT = sb("pT", [P, 2, TB])
        row = [sb(f"row{j}", [P, 2, RW]) for j in range(2)]
        stats2, mean_var2 = sb("stats2", [P, 2, 6]), sb("mean_var2", [P, 2, 2])
        var_eps2 = sb("var_eps2", [P, 2])
        xn2 = sb("xn2", [P, 2, D])
        x2T = sb("x2T", [P, DC, TB])
        lmax, shifted, lexp = sb("lmax", [P, 2]), sb("shifted", [P, 2, E]), sb("lexp", [P, 2, E])
        ranked, rmax = sb("ranked", [P, 2, E]), sb("rmax", [P, 2])
        chosen = sb("chosen", [P, 2, E], bf16)
        both = sb("both", [P, E], bf16)
        before = [sb(f"before{j}", [P, E], bf16) for j in range(2)]
        gsum = sb("gsum", [P, 2])
        counted, loc, over, place = sb("counted", [P, 2, E]), sb("loc", [P, 2]), sb("over", [P, 2]), sb("place", [P, 2])
        slot = [sb(f"slot{j}", [P, 2], i32) for j in range(2)]
        empty = sb("empty", [P, RW])
        xs = [sb(f"xs{j}", [P, 2, D]) for j in range(2)]
        xg_high, xg_low = ([sb(f"xg_{n}{j}", [P, DC, CAP], f32r) for j in range(2)] for n in ("high", "low"))
        w1_high, w1_low = ([sb(f"w1_{n}{j}", [P, DC, F], f32r) for j in range(2)] for n in ("high", "low"))
        w2_high, w2_low = ([sb(f"w2_{n}{j}", [P, FC, D], f32r) for j in range(2)] for n in ("high", "low"))
        h_high, h_low = ([sb(f"h_{n}{j}", [P, FC, CAP], f32r) for j in range(2)] for n in ("high", "low"))
        y = [sb(f"y{j}", [P, 2, D]) for j in range(2)]
        goal = [sb(f"goal{j}", [P, 2], i32) for j in range(2)]

        banks = [bank(f"bank{j}") for j in range(8)]

        def halves(j):
            return banks[j][:, :].rearrange("p (a b) -> p a b", a=2)

        ps_xT, ps_q, ps_s, ps_v, ps_pT, ps_o, ps_x2T = (halves(j) for j in range(7))
        ps_logit = banks[7][:, 0:2 * E].rearrange("p (a b) -> p a b", a=2)
        ps_count = banks[7][:, 2 * E:4 * E].rearrange("p (a b) -> p a b", a=2)
        ps_h = [halves(n) for n in range(FC // 2)]
        ps_gT = halves(6)
        ps_y = [halves(4), halves(5)]

        const_in, eye_in, weights_in, small_in = sem("const_in"), sem("eye_in"), sem("weights_in"), sem("small_in")
        x_in = [sem(f"x_in{j}") for j in range(4)]
        w1_in, w2_in = sem("w1_in"), sem("w2_in")
        w1_high_ready, w1_split, w2_high_ready, w2_split = (sem(n) for n in ("w1_high_ready", "w1_split", "w2_high_ready", "w2_split"))
        row_free, y_free = sem("row_free"), sem("y_free")
        slots_in = [sem(f"slots_in{j}") for j in range(2)]
        x2_stored = [sem(f"x2_stored{j}") for j in range(2)]
        row_sent = [sem(f"row_sent{j}") for j in range(2)]
        y_sent = [sem(f"y_sent{j}") for j in range(2)]
        slots_empty, empty_ready = sem("slots_empty"), sem("empty_ready")
        tables = sem("tables")
        setup_step = sem("setup_step")
        fold_a, fold_wo, fold_m, fold_b = sem("fold_a"), sem("fold_wo"), sem("fold_m"), sem("fold_b")
        a_ready, wo_ready, m_ready, b_ready = sem("a_ready"), sem("wo_ready"), sem("m_ready"), sem("b_ready")
        var_ready, rstd_ready, nmr_ready = sem("var_ready"), sem("rstd_ready"), sem("nmr_ready")
        xn_ready, xb_ready = sem("xn_ready"), sem("xb_ready")
        xT_made, xT_ready = sem("xT_made"), sem("xT_ready")
        q_made, q_ready = sem("q_made"), sem("q_ready")
        s_made, top_ready = sem("s_made"), sem("top_ready")
        v_made, v_ready = sem("v_made"), sem("v_ready")
        e_ready, prob_ready = sem("e_ready"), sem("prob_ready")
        pT_made, pT_ready = sem("pT_made"), sem("pT_ready")
        o_made, x2_ready = sem("o_made"), sem("x2_ready")
        var2_ready, rstd2_ready, xn2_ready = sem("var2_ready"), sem("rstd2_ready"), sem("xn2_ready")
        x2T_made, x2T_ready = sem("x2T_made"), sem("x2T_ready")
        logit_made, shifted_ready, lexp_ready = sem("logit_made"), sem("shifted_ready"), sem("lexp_ready")
        chosen_ready, count_made, slot_ready = sem("chosen_ready"), sem("count_made"), sem("slot_ready")
        token_ready = sem("token_ready")
        attn_step, norm_step = sem("attn_step"), sem("norm_step")
        choose_step, place_step, total_step = sem("choose_step"), sem("place_step"), sem("total_step")
        xs_ready, gT_made, gT_ready = sem("xs_ready"), sem("gT_made"), sem("gT_ready")
        xg_split, h_made, h_high_ready, h_split = sem("xg_split"), sem("h_made"), sem("h_high_ready"), sem("h_split")
        y_made, y_ready = sem("y_made"), [sem(f"y_ready{j}") for j in range(2)]
        goal_ready = sem("goal_ready")

        pool_passed, dve_passed = sem("pool_passed"), sem("dve_passed")
        block = ctx.enter_context(nc.Block())
        x_view = x.rearrange("b h w d -> (b h w) d").rearrange("(t p) d -> p t d", p=P)
        out_rows = out.rearrange("b h w d -> (b h w) d")
        out_view = out_rows.rearrange("(t p) d -> p t d", p=P)
        slots_view = slots.rearrange("(t p) r -> p t r", p=P)
        w1_view = w1.rearrange("e (c p) f -> e p c f", p=P)
        w2_view = w2.rearrange("e (c p) d -> e p c d", p=P)

        def matrix(w):
            return w.rearrange("(c p) d -> p c d", p=P)

        def pairs(eng, first, last, body):
            assert (last - first) % 2 == 1
            with eng.Fori(0, (last - first + 1) // 2) as turn:
                for step in range(2):
                    n = first + step
                    body(turn + n // 2, n % 2)

        def peeled(n, body, **how):
            body(n // 2, n % 2, **how)

        @block.sync
        def _(sp):
            sp.dma_start(x_sb[:, 0:4, :], x_view[:, 0:4, :]).then_inc(x_in[0], 16)
            sp.dma_start(wk_sb, matrix(Wk)).then_inc(weights_in, 16)
            sp.dma_start(wv_sb, matrix(Wv)).then_inc(weights_in, 16)
            for g in range(1, 4):
                sp.dma_start(x_sb[:, 4 * g:4 * g + 4, :], x_view[:, 4 * g:4 * g + 4, :]).then_inc(x_in[g], 16)
            sp.sem_inc(row_free, 4)
            sp.wait_ge(xT_made, 1)
            sp.wait_ge(empty_ready, 1)
            sp.dma_start(slots_view, empty[:, None, :].to_broadcast([P, NT, RW])).then_inc(slots_empty, 16)
            sp.dma_start(w1_in_sb[:, :, :], w1_view[0]).then_inc(w1_in, 16)
            sp.wait_ge(fold_m, 1)
            sp.dma_start(w2_in_sb[:, :, :], w2_view[0]).then_inc(w2_in, 16)

            def store_x2(k, j):
                sp.wait_ge(x2_ready, 2 * k + j + 1)
                sp.dma_start(out_view[:, bass.ds(4 * k + 2 * j, 2), :], row[j][:, :, 0:D]).then_inc(x2_stored[j], 16)
                sp.wait_ge(x2_stored[j], 16 * (k + 1))
                sp.sem_inc(row_free, 1)
                sp.wait_ge(row_sent[j], 32 * (k + 1))
                sp.sem_inc(row_free, 1)

            peeled(0, store_x2)
            sp.wait_ge(w1_split, 1)
            sp.dma_start(w1_in_sb[:, :, :], w1_view[1]).then_inc(w1_in, 16)
            sp.wait_ge(w2_split, 1)
            sp.dma_start(w2_in_sb[:, :, :], w2_view[1]).then_inc(w2_in, 16)
            pairs(sp, 1, B - 2, store_x2)
            peeled(B - 1, store_x2)

            def load_slots(k, j):
                wait(sp, slots_in[j], 16 * k)
                sp.dma_start(sl[:, bass.ds(4 * k + 2 * j, 2), :], slots_view[:, bass.ds(4 * k + 2 * j, 2), :]).then_inc(slots_in[j], 16)

            peeled(0, load_slots)
            peeled(1, load_slots)
            sp.wait_ge(w1_split, 2)
            sp.dma_start(w1_in_sb[:, :, :], w1_view[2]).then_inc(w1_in, 16)
            pairs(sp, 2, E - 1, load_slots)
            sp.sem_inc(y_free, 2)

            def load_weights(k, j, w1_too=True):
                e = 2 * k + j
                sp.wait_ge(w2_split, e)
                sp.dma_start(w2_in_sb[:, :, :], w2_view[e]).then_inc(w2_in, 16)
                if w1_too:
                    sp.wait_ge(w1_split, e + 1)
                    sp.dma_start(w1_in_sb[:, :, :], w1_view[e + 1]).then_inc(w1_in, 16)
                sp.wait_ge(y_sent[j], 32 * k)
                sp.sem_inc(y_free, 1)

            pairs(sp, 2, E - 3, load_weights)
            peeled(E - 2, load_weights)
            peeled(E - 1, load_weights, w1_too=False)
            for j in range(2):
                sp.wait_ge(y_sent[j], 32 * (E // 2))

        @block.gpsimd
        def _(pool):
            nc.gpsimd.memset(empty[:, :], 0.0).then_inc(token_ready, 1)
            pool.wait_ge(token_ready, 1)
            nc.gpsimd.memset(empty[:, COL_TOK:COL_TOK + 1].bitcast(i32), NOWHERE).then_inc(empty_ready, 1)
            for g, (a, b) in enumerate(((0, 4), (4, NT))):
                pool.wait_ge(var_ready, g + 1)
                nc.gpsimd.tensor_tensor(rstd[:, a:b], var_eps[:, a:b], minus_half[:, a:b], ALU.pow).then_inc(rstd_ready, 1)
            pool.wait_ge(b_ready, 1)
            def scatter_rows(k, j):
                wait_apart(pool, slot_ready, 2 * k + j + 1, pool_passed)
                for t in range(2):
                    nc.gpsimd.indirect_dma_start(
                        slots, bass.IndirectOffsetOnAxis(ap=slot[j][:, t:t + 1].bitcast(u32), axis=0),
                        row[j][:, t, :], None, bounds_check=N - 1, oob_is_err=False).then_inc(row_sent[j], 16)

            def batch(k, j, before_it=True):
                i = 2 * k + j
                nc.gpsimd.tensor_tensor(xb[j][:, :, :], x_sb[:, bass.ds(4 * k + 2 * j, 2), :],
                                        obias[:, None, :].to_broadcast([P, 2, D]), ALU.add).then_inc(xb_ready, 1)
                pool.wait_ge(var2_ready, i + 1)
                nc.gpsimd.tensor_tensor(row[j][:, :, COL_RSTD], var_eps2[:, :], minus_half[:, 0:2], ALU.pow).then_inc(rstd2_ready, 1)
                if before_it:
                    scatter_rows(*((k, 0) if j == 1 else (k - 1, 1)))

            def split_w2(n, j):
                pool.wait_ge(w2_high_ready, n + 1)
                for part in range(2):
                    half = slice(part * FC // 2, (part + 1) * FC // 2)
                    step = nc.gpsimd.tensor_tensor(w2_low[j][:, half, :], w2_in_sb[:, half, :], w2_high[j][:, half, :].bitcast(f32), ALU.subtract)
                step.then_inc(w2_split, 1)

            peeled(0, batch, before_it=False)
            split_w2(0, 0)
            pool.wait_ge(slots_empty, 16)
            pairs(pool, 1, B - 2, batch)
            peeled(B - 1, batch)
            scatter_rows(B // 2 - 1, 1)

            for j in range(2):
                pool.wait_ge(x2_stored[j], 16 * (B // 2))

            def scatter_y(k, j):
                wait_apart(pool, y_ready[j], k + 1, pool_passed)
                for c in range(2):
                    nc.gpsimd.indirect_dma_start(
                        out_rows, bass.IndirectOffsetOnAxis(ap=goal[j][:, c:c + 1].bitcast(u32), axis=0),
                        y[j][:, c, :], None, bounds_check=N - 1, oob_is_err=False).then_inc(y_sent[j], 16)

            def expert(k, j):
                split_w2(2 * k + j + 1, 1 - j)
                scatter_y(k, j)

            pairs(pool, 0, E - 3, expert)
            peeled(E - 2, expert)
            peeled(E - 1, scatter_y)

        @block.tensor
        def _(pe):
            pe.wait_ge(weights_in, 64)
            for d in range(DC):
                for c in range(DC):
                    step = nc.tensor.matmul(ps_q[:, d, :], wq_sb[:, c, d * P:(d + 1) * P], wk_sb[:, c, :], start=c == 0, stop=c == DC - 1)
            step.then_inc(fold_a, 1)
            pe.wait_ge(eye_in, 16)
            for c in range(DC):
                for m in range(DC):
                    step = nc.tensor.transpose(ps_s[:, m, c * P:(c + 1) * P], wo_sb[:, c, m * P:(m + 1) * P], ident)
            step.then_inc(fold_wo, 1)
            pe.wait_ge(small_in, 80)
            for d in range(DC):
                for c in range(DC):
                    step = nc.tensor.matmul(banks[7][:, 4 * E + d:4 * E + d + 1], wk_sb[:, c, d * P:(d + 1) * P], bq_sb[:, c:c + 1], start=c == 0, stop=c == DC - 1)
            step.then_inc(fold_b, 1)

            def transpose_x(k, j):
                i = 2 * k + j
                pe.wait_ge(xn_ready, i + 1)
                wait(pe, xT_ready, i)
                for t in range(2):
                    for c in range(DC):
                        step = nc.tensor.transpose(ps_xT[:, c, t * P:(t + 1) * P], xn[:, t, c * P:(c + 1) * P], ident)
                step.then_inc(xT_made, 1)

            def query(k, j):
                i = 2 * k + j
                pe.wait_ge(xT_ready, i + 1)
                wait(pe, q_ready, 2 * i)
                for d in range(DC):
                    for c in range(DC):
                        step = nc.tensor.matmul(ps_q[:, d, :], a_sb[:, c, d * P:(d + 1) * P], xT[j][:, c, :], start=c == 0, stop=c == DC - 1)
                step.then_inc(q_made, 1)

            def batch(k, j, before_it=True, next_one=True):
                i = 2 * k + j
                kn, jn = (k, 1) if j == 0 else (k + 1, 0)
                pe.wait_ge(q_ready, 2 * i + 2)
                wait(pe, top_ready, i)
                for t in range(2):
                    for c in range(DC):
                        step = nc.tensor.matmul(ps_s[:, t, :], qT[j][:, c, t * P:(t + 1) * P], xT[j][:, c, :], start=c == 0, stop=c == DC - 1)
                step.then_inc(s_made, 1)
                wait(pe, v_ready, i)
                for t in range(2):
                    for c in range(DC):
                        step = nc.tensor.matmul(ps_v[:, t, :], xT[j][:, c, t * P:(t + 1) * P], mT[:, c, :], start=c == 0, stop=c == DC - 1)
                step.then_inc(v_made, 1)
                if next_one:
                    transpose_x(kn, jn)
                if before_it:
                    transpose_x2(i - 1)
                if next_one:
                    query(kn, jn)
                pe.wait_ge(prob_ready, i + 1)
                wait(pe, pT_ready, i)
                for t in range(2):
                    for c in range(2):
                        step = nc.tensor.transpose(ps_pT[:, c, t * P:(t + 1) * P], prob[:, t, c * P:(c + 1) * P], ident)
                step.then_inc(pT_made, 1)
                if before_it:
                    logits(i - 1)
                pe.wait_ge(pT_ready, i + 1)
                pe.wait_ge(v_ready, i + 1)
                wait(pe, x2_ready, i)
                for t in range(2):
                    for c in range(2):
                        step = nc.tensor.matmul(ps_o[:, t, :], pT[:, c, t * P:(t + 1) * P], v_sb[:, c, :], start=c == 0, stop=c == 1)
                    if t == 0 and before_it:
                        counts(i - 1, 1 - j)
                step.then_inc(o_made, 1)

            def transpose_x2(i):
                pe.wait_ge(xn2_ready, i + 1)
                for t in range(2):
                    for c in range(DC):
                        step = nc.tensor.transpose(ps_x2T[:, c, t * P:(t + 1) * P], xn2[:, t, c * P:(c + 1) * P], ident)
                step.then_inc(x2T_made, 1)

            def logits(i):
                pe.wait_ge(x2T_ready, i + 1)
                for t in range(2):
                    for c in range(DC):
                        step = nc.tensor.matmul(ps_logit[:, t, :], x2T[:, c, t * P:(t + 1) * P], wg_sb[:, c, :], start=c == 0, stop=c == DC - 1)
                step.then_inc(logit_made, 1)

            def counts(i, j):
                pe.wait_ge(chosen_ready, i + 1)
                nc.tensor.matmul(ps_count[:, 0, :], upper[:, :], chosen[:, 0, :], start=True, stop=False)
                nc.tensor.matmul(ps_count[:, 0, :], ones[:, :], before[j][:, :], start=False, stop=True)
                nc.tensor.matmul(ps_count[:, 1, :], upper[:, :], chosen[:, 1, :], start=True, stop=False)
                nc.tensor.matmul(ps_count[:, 1, :], ones[:, :], chosen[:, 0, :], start=False, stop=False)
                nc.tensor.matmul(ps_count[:, 1, :], ones[:, :], before[j][:, :], start=False, stop=True).then_inc(count_made, 1)

            peeled(0, transpose_x)
            pe.wait_ge(wo_ready, 1)
            for d in range(DC):
                for m in range(DC):
                    step = nc.tensor.matmul(ps_v[:, d, :], wv_sb[:, m, d * P:(d + 1) * P], woT[:, m, :], start=m == 0, stop=m == DC - 1)
            step.then_inc(fold_m, 1)
            pe.wait_ge(tables, 1)
            for m in range(DC):
                step = nc.tensor.matmul(banks[5][:, 0:D], bv_wide[:, m, :], woT[:, m, :], start=m == 0, stop=m == DC - 1)
            step.then_inc(fold_b, 1)
            pe.wait_ge(a_ready, 1)
            peeled(0, query)
            pe.wait_ge(m_ready, 1)
            pe.wait_ge(b_ready, 1)
            pe.wait_ge(tables, 2)
            peeled(0, batch, before_it=False)
            pairs(pe, 1, B - 2, batch)
            peeled(B - 1, batch, next_one=False)
            transpose_x2(B - 1)
            logits(B - 1)
            counts(B - 1, (B - 1) % 2)

            def gather_T(k, j):
                e = 2 * k + j
                pe.wait_ge(xs_ready, e + 1)
                wait(pe, xg_split, e)
                for t in range(2):
                    for c in range(DC):
                        step = nc.tensor.transpose(ps_gT[:, c, t * P:(t + 1) * P], xs[j][:, t, c * P:(c + 1) * P], ident)
                step.then_inc(gT_made, 1)

            def three_passes(out_ap, stationary, moving, start, stop):
                (a_high, a_low), (b_high, b_low) = stationary, moving
                nc.tensor.matmul(out_ap, a_high, b_high, start=start, stop=False)
                nc.tensor.matmul(out_ap, a_high, b_low, start=False, stop=False)
                return nc.tensor.matmul(out_ap, a_low, b_high, start=False, stop=stop)

            def hidden(k, j):
                e = 2 * k + j
                pe.wait_ge(w1_split, e + 1)
                pe.wait_ge(xg_split, e + 1)
                for q in range(FC // 2):
                    wait(pe, h_split, (FC // 2) * (e - 1) + q + 1)
                    for u in range(2):
                        f = slice((2 * q + u) * P, (2 * q + u + 1) * P)
                        for c in range(DC):
                            step = three_passes(ps_h[q][:, u, :], (w1_high[j][:, c, f], w1_low[j][:, c, f]),
                                                (xg_high[j][:, c, :], xg_low[j][:, c, :]), c == 0, c == DC - 1)
                    step.then_inc(h_made, 1)

            def expert_out(k, j):
                e = 2 * k + j
                pe.wait_ge(w2_split, e + 1)
                pe.wait_ge(h_split, (FC // 2) * (e + 1))
                for t in range(2):
                    own = slice(t * P, (t + 1) * P)
                    for f in range(FC):
                        step = three_passes(ps_y[j][:, t, :], (h_high[j][:, f, own], h_low[j][:, f, own]),
                                            (w2_high[j][:, f, :], w2_low[j][:, f, :]), f == 0, f == FC - 1)
                step.then_inc(y_made, 1)

            def expert(k, j, two_on=True):
                hidden(*((k, 1) if j == 0 else (k + 1, 0)))
                if two_on:
                    gather_T(k + 1, j)
                expert_out(k, j)

            peeled(0, gather_T)
            peeled(1, gather_T)
            peeled(0, hidden)
            pairs(pe, 0, E - 3, expert)
            peeled(E - 2, expert, two_on=False)
            pe.wait_ge(y_ready[1], E // 2 - 1)
            peeled(E - 1, expert_out)

        @block.scalar
        def _(act):
            act.dma_start(wq_sb, matrix(Wq)).then_inc(weights_in, 16)
            act.dma_start(ident_sb[:, :], eye).then_inc(eye_in, 16)
            act.dma_start(wo_sb, matrix(Wo)).then_inc(weights_in, 16)
            with nc.allow_non_contiguous_dma(reason="bias columns of 128"):
                act.dma_start(bq_sb[:, :], bq.rearrange("(c p) -> p c", p=P)).then_inc(small_in, 16)
                act.dma_start(bv_sb[:, :], bv.rearrange("(c p) -> p c", p=P)).then_inc(small_in, 16)
            act.dma_start(sigma_sb[:, :], sigma[None, :].to_broadcast([P, 1])).then_inc(small_in, 16)
            act.dma_start(bo_sb[:, :], bo[None, :].to_broadcast([P, D])).then_inc(small_in, 16)
            act.dma_start(wg_sb[:, :, :], wg.rearrange("(c p) e -> p c e", p=P)).then_inc(small_in, 16)
            act.dma_start(table[:, :], tables_in).then_inc(const_in, 16)
            act.dma_start(token[:, :], tokens).then_inc(const_in, 16)

            def normalised_x(k, j):
                i = 2 * k + j
                wait(act, xT_made, i)
                for t in range(2):
                    r = 4 * k + 2 * j + t
                    step = nc.scalar.activation(xn[:, t, :], x_sb[:, bass.ds(r, 1), :], ACT.Identity,
                                                scale=rstd[:, bass.ds(r, 1)], bias=nmr[:, bass.ds(r, 1)])
                step.then_inc(xn_ready, 1)

            act.wait_ge(nmr_ready, 1)
            peeled(0, normalised_x)
            act.wait_ge(fold_a, 1)
            nc.scalar.activation(a_sb[:, :, :], ps_q, ACT.Copy).then_inc(a_ready, 1)
            act.wait_ge(fold_wo, 1)
            nc.scalar.activation(woT[:, :, :], ps_s, ACT.Copy).then_inc(wo_ready, 1)
            act.wait_ge(fold_m, 1)
            nc.scalar.activation(mT[:, :, :], ps_v, ACT.Copy).then_inc(m_ready, 1)
            act.wait_ge(b_ready, 1)
            act.wait_ge(nmr_ready, 2)

            def query(k, j):
                i = 2 * k + j
                act.wait_ge(q_made, i + 1)
                for d in range(DC):
                    nc.scalar.activation(qT[j][:, d, :], ps_q[:, d, :], ACT.Identity, bias=qbias[:, d:d + 1]).then_inc(q_ready, 1)

            def batch(k, j, before_it=True, next_one=True):
                i = 2 * k + j
                if next_one:
                    normalised_x(*((k, 1) if j == 0 else (k + 1, 0)))
                act.wait_ge(top_ready, i + 1)
                for t in range(2):
                    nc.scalar.activation(e_col[:, t, :], s_col[:, t, :], ACT.Exp, bias=ntop[:, t:t + 1], accum_out=esum[:, t:t + 1]).then_inc(e_ready, 1)
                    nc.scalar.activation(e_row[:, t, :], s_row[:, t, :], ACT.Exp, bias=ntop[:, 2 + t:3 + t], accum_out=esum[:, 2 + t:3 + t]).then_inc(e_ready, 1)
                if before_it:
                    transposed_x2(i - 1)
                act.wait_ge(v_made, i + 1)
                wait(act, o_made, i)
                nc.scalar.activation(v_sb[:, :, :], ps_v, ACT.Copy).then_inc(v_ready, 1)
                if next_one:
                    query(*((k, 1) if j == 0 else (k + 1, 0)))
                act.wait_ge(pT_made, i + 1)
                nc.scalar.activation(pT[:, :, :], ps_pT, ACT.Copy).then_inc(pT_ready, 1)
                if before_it:
                    gate_exp(i - 1)

            def transposed_x2(i):
                act.wait_ge(x2T_made, i + 1)
                nc.scalar.activation(x2T[:, :, :], ps_x2T, ACT.Copy).then_inc(x2T_ready, 1)

            def gate_exp(i):
                act.wait_ge(shifted_ready, i + 1)
                nc.scalar.activation(lexp[:, :, :], shifted[:, :, :], ACT.Exp).then_inc(lexp_ready, 1)

            def split_w(high, loaded, raw, ready, n, j):
                act.wait_ge(loaded, 16 * (n + 1))
                parts = raw.shape[1] // 2
                for part in range(2):
                    half = slice(part * parts, (part + 1) * parts)
                    step = nc.scalar.activation(high[j][:, half, :], raw[:, half, :], ACT.Copy)
                step.then_inc(ready, 1)

            def split_w1(n, j):
                split_w(w1_high, w1_in, w1_in_sb, w1_high_ready, n, j)

            def split_w2(n, j):
                split_w(w2_high, w2_in, w2_in_sb, w2_high_ready, n, j)

            peeled(0, query)
            peeled(0, batch, before_it=False)
            split_w1(0, 0)
            split_w2(0, 0)
            pairs(act, 1, B - 2, batch)
            peeled(B - 1, batch, next_one=False)
            transposed_x2(B - 1)
            gate_exp(B - 1)

            def gathered_T(k, j):
                act.wait_ge(gT_made, 2 * k + j + 1)
                nc.scalar.activation(xg_high[j][:, :, :], ps_gT, ACT.Copy).then_inc(gT_ready, 1)

            def hidden(k, j, w2_next=None):
                e = 2 * k + j
                for q in range(FC // 2):
                    act.wait_ge(h_made, (FC // 2) * e + q + 1)
                    nc.scalar.activation(h_high[j][:, 2 * q:2 * q + 2, :], ps_h[q], ACT.Relu).then_inc(h_high_ready, 1)
                    if q == 1 and w2_next:
                        split_w2(*w2_next)

            def expert(k, j, two_on=True):
                e = 2 * k + j
                hidden(*((k, 1) if j == 0 else (k + 1, 0)), w2_next=(e + 1, 1 - j))
                if two_on:
                    gathered_T(k + 1, j)
                    split_w1(e + 2, j)

            split_w1(1, 1)
            peeled(0, gathered_T)
            peeled(1, gathered_T)
            peeled(0, hidden)
            pairs(act, 0, E - 3, expert)
            peeled(E - 2, expert, two_on=False)

        @block.vector
        def _(dve):
            setup = Chain(dve, setup_step, 0, None)
            nc.vector.memset(minus_half[:, :], -0.5)
            nc.vector.memset(before[0][:, :], 0.0)
            setup.mark(nc.vector.memset(ones[:, :], 1.0))
            setup.done(nc.vector.memset(bv_wide[:, :, :], 1.0))

            def first_norm(a, b):
                for i in range(a, b):
                    if i % 4 == 0:
                        dve.wait_ge(x_in[i // 4], 16)
                    setup.mark(nc.vector.bn_stats(stats[:, i, :], x_sb[:, i, :]))
                setup.done()
                for i in range(a, b):
                    setup.mark(nc.vector.bn_aggr(mean_var[:, i, :], stats[:, i, :]))
                setup.done()
                nc.vector.tensor_scalar(var_eps[:, a:b], mean_var[:, a:b, 1], EPS_C, None, ALU.add).then_inc(var_ready, 1)

            def first_norm_offsets(g, a, b):
                dve.wait_ge(rstd_ready, g + 1)
                nc.vector.scalar_tensor_tensor(nmr[:, a:b], mean_var[:, a:b, 0], -1.0, rstd[:, a:b], ALU.mult, ALU.mult).then_inc(nmr_ready, 1)

            first_norm(0, 4)
            first_norm_offsets(0, 0, 4)
            dve.wait_ge(small_in, 80)
            for c in range(DC):
                step = nc.vector.tensor_scalar(bv_wide[:, c, :], bv_wide[:, c, :], bv_sb[:, c:c + 1], None, ALU.mult)
            step.then_inc(tables, 1)
            dve.wait_ge(const_in, 32)
            setup.mark(nc.vector.tensor_scalar(mask_row[:, :], far_row, OFF, None, ALU.mult))
            for t in range(2):
                setup.mark(nc.vector.tensor_scalar(mask_col[:, t * TB:(t + 1) * TB], far_col, OFF, None, ALU.mult))
            setup.mark(nc.vector.tensor_copy(upper[:, :], upper_in))
            setup.done(nc.vector.tensor_tensor(decay[:, 0:1], sigma_sb[:, :], sigma_sb[:, :], ALU.mult))
            setup.done(nc.vector.reciprocal(decay[:, 1:2], decay[:, 0:1]))
            setup.done(nc.vector.tensor_scalar(decay[:, 0:1], decay[:, 1:2], -0.5, None, ALU.mult))
            setup.mark(nc.vector.scalar_tensor_tensor(mask_row[:, :], dist_row, decay[:, 0:1], mask_row[:, :], ALU.mult, ALU.add))
            setup.mark(nc.vector.scalar_tensor_tensor(mask_col[:, :], dist_col, decay[:, 0:1], mask_col[:, :], ALU.mult, ALU.add))
            dve.wait_ge(fold_b, 1)
            nc.vector.tensor_copy(qbias[:, :], banks[7][:, 4 * E:4 * E + DC]).then_inc(tables, 1)

            def transposed_x(k, j):
                i = 2 * k + j
                dve.wait_ge(xT_made, i + 1)
                wait(dve, v_made, i - 1)
                wait(dve, s_made, i - 1)
                nc.vector.tensor_copy(xT[j][:, :, :], ps_xT).then_inc(xT_ready, 1)

            peeled(0, transposed_x)
            dve.wait_ge(fold_b, 2)
            nc.vector.scalar_tensor_tensor(obias[:, :], banks[5][:, 0:D], 2.0, bo_sb[:, :], ALU.mult, ALU.add).then_inc(b_ready, 1)
            first_norm(4, NT)
            first_norm_offsets(1, 4, NT)
            dve.wait_ge(nmr_ready, 2)

            def maxima(k, j):
                i = 2 * k + j
                chain = Chain(dve, attn_step, 8 * i, 5)
                wait_apart(dve, s_made, i + 1, dve_passed)
                for t in range(2):
                    chain.mark(nc.vector.tensor_tensor_reduce(
                        out=s_col[:, t, :], in0=ps_s[:, t, :], in1=mask_col[:, t * TB:(t + 1) * TB], scale=1.0,
                        scalar=-3e38, op0=ALU.add, op1=ALU.max, accum_out=top[:, t:t + 1]))
                    chain.mark(nc.vector.tensor_tensor_reduce(
                        out=s_row[:, t, :], in0=ps_s[:, t, t * P:(t + 1) * P], in1=mask_row[:, :], scale=1.0,
                        scalar=-3e38, op0=ALU.add, op1=ALU.max, accum_out=top[:, 2 + t:3 + t]))
                chain.done()
                nc.vector.tensor_scalar(ntop[:, :], top[:, :], -1.0, None, ALU.mult).then_inc(top_ready, 1)

            def probabilities(k, j):
                i = 2 * k + j
                chain = Chain(dve, attn_step, 8 * i + 4, 3)
                dve.wait_ge(e_ready, 4 * i + 4)
                chain.done(nc.vector.reciprocal(einv[:, :], esum[:, :]))
                wait(dve, pT_made, i)
                for t in range(2):
                    chain.mark(nc.vector.tensor_scalar(prob[:, t, :], e_col[:, t, :], einv[:, t:t + 1], None, ALU.mult))
                chain.done()
                own = [prob[:, t, t * P:(t + 1) * P] for t in range(2)]
                nc.vector.scalar_tensor_tensor(own[0], e_row[:, 0, :], einv[:, 2:3], own[0], ALU.mult, ALU.add).then_inc(attn_step, 1)
                nc.vector.scalar_tensor_tensor(own[1], e_row[:, 1, :], einv[:, 3:4], own[1], ALU.mult, ALU.add).then_inc(prob_ready, 1)

            def residual(k, j):
                i = 2 * k + j
                chain = Chain(dve, norm_step, 5 * i, 4)
                dve.wait_ge(o_made, i + 1)
                dve.wait_ge(xb_ready, i + 1)
                dve.wait_ge(row_free, 2 * i + 2)
                nc.vector.tensor_tensor(row[j][:, :, 0:D], ps_o, xb[j][:, :, :], ALU.add).then_inc(x2_ready, 1)
                dve.wait_ge(x2_ready, i + 1)
                for t in range(2):
                    chain.mark(nc.vector.bn_stats(stats2[:, t, :], row[j][:, t, 0:D]))
                chain.done()
                dve.sem_inc(dve_passed, 1)
                for t in range(2):
                    chain.mark(nc.vector.bn_aggr(mean_var2[:, t, :], stats2[:, t, :]))
                chain.done()
                nc.vector.tensor_scalar(var_eps2[:, :], mean_var2[:, :, 1], EPS_T, None, ALU.add).then_inc(var2_ready, 1)

            def normalised(k, j):
                i = 2 * k + j
                chain = Chain(dve, norm_step, 5 * i + 4, 1)
                dve.wait_ge(rstd2_ready, i + 1)
                chain.done(nc.vector.scalar_tensor_tensor(row[j][:, :, COL_NMR], mean_var2[:, :, 0], -1.0, row[j][:, :, COL_RSTD], ALU.mult, ALU.mult))
                for t in range(2):
                    step = nc.vector.tensor_scalar(xn2[:, t, :], row[j][:, t, 0:D], row[j][:, t, COL_RSTD:COL_RSTD + 1],
                                                   row[j][:, t, COL_NMR:COL_NMR + 1], ALU.mult, ALU.add)
                step.then_inc(xn2_ready, 1)

            def wide(a):
                return a.unsqueeze(2).to_broadcast([P, 2, E])

            def choose(k, j):
                i = 2 * k + j
                chain = Chain(dve, choose_step, 4 * i, 4)
                dve.wait_ge(logit_made, i + 1)
                chain.done(nc.vector.tensor_reduce(lmax[:, :], ps_logit, axis=AX.X, op=ALU.max))
                nc.vector.tensor_tensor(shifted[:, :, :], ps_logit, wide(lmax[:, :]), ALU.subtract).then_inc(shifted_ready, 1)
                dve.wait_ge(shifted_ready, i + 1)
                chain.done(nc.vector.scalar_tensor_tensor(ranked[:, :, :], shifted[:, :, :], 0.0, rank, ALU.is_equal, ALU.mult))
                chain.done(nc.vector.tensor_reduce(rmax[:, :], ranked[:, :, :], axis=AX.X, op=ALU.max))
                nc.vector.tensor_tensor(chosen[:, :, :], rank, wide(rmax[:, :]), ALU.is_equal).then_inc(chosen_ready, 1)
                chain.mark(nc.vector.tensor_copy(row[j][:, :, COL_TOK].bitcast(i32), token[:, bass.ds(4 * k + 2 * j, 2)]))
                chain.close()

            def running_totals(k, j):
                i = 2 * k + j
                chain = Chain(dve, total_step, 2 * i, 2)
                chain.done(nc.vector.tensor_tensor(both[:, :], chosen[:, 0, :], chosen[:, 1, :], ALU.add))
                chain.mark(nc.vector.tensor_tensor(before[1 - j][:, :], before[j][:, :], both[:, :], ALU.add))
                chain.close()

            def place_rows(k, j):
                i = 2 * k + j
                chain = Chain(dve, place_step, 6 * i, 6)
                dve.wait_ge(lexp_ready, i + 1)
                chain.mark(nc.vector.tensor_reduce(gsum[:, :], lexp[:, :, :], axis=AX.X, op=ALU.add))
                dve.wait_ge(count_made, i + 1)
                chain.done(nc.vector.tensor_tensor(counted[:, :, :], ps_count, chosen[:, :, :], ALU.mult))
                chain.mark(nc.vector.reciprocal(row[j][:, :, COL_GATE], gsum[:, :]))
                chain.done(nc.vector.tensor_reduce(loc[:, :], counted[:, :, :], axis=AX.X, op=ALU.add))
                chain.mark(nc.vector.tensor_scalar(over[:, :], loc[:, :], float(CAP), float(NOWHERE), ALU.is_gt, ALU.mult))
                chain.done(nc.vector.scalar_tensor_tensor(place[:, :], rmax[:, :], -float(CAP), loc[:, :], ALU.mult, ALU.add))
                nc.vector.scalar_tensor_tensor(slot[j][:, :], place[:, :], float(CAP * E - 1), over[:, :], ALU.add, ALU.add).then_inc(slot_ready, 1)
                chain.close()

            def batch(k, j, before_it=True, next_one=True):
                kb, jb = (k, 0) if j == 1 else (k - 1, 1)
                if before_it:
                    residual(kb, jb)
                maxima(k, j)
                if before_it:
                    normalised(kb, jb)
                if next_one:
                    transposed_x(*((k, 1) if j == 0 else (k + 1, 0)))
                probabilities(k, j)
                if before_it:
                    choose(kb, jb)
                    place_rows(kb, jb)
                    running_totals(kb, jb)

            def gathered(k, j):
                e = 2 * k + j
                dve.wait_ge(slots_in[j], 16 * (k + 1))
                for t in range(2):
                    r = 4 * k + 2 * j + t
                    step = nc.vector.tensor_scalar(xs[j][:, t, :], sl[:, bass.ds(r, 1), 0:D], sl[:, bass.ds(r, 1), COL_RSTD:COL_RSTD + 1],
                                                   sl[:, bass.ds(r, 1), COL_NMR:COL_NMR + 1], ALU.mult, ALU.add)
                step.then_inc(xs_ready, 1)

            def output_rows(k, j):
                e = 2 * k + j
                dve.wait_ge(y_free, e + 1)
                nc.vector.tensor_copy(goal[j][:, :], sl[:, bass.ds(4 * k + 2 * j, 2), COL_TOK].bitcast(i32)).then_inc(goal_ready, 1)
                dve.wait_ge(y_made, e + 1)
                for t in range(2):
                    r = 4 * k + 2 * j + t
                    step = nc.vector.scalar_tensor_tensor(y[j][:, t, :], ps_y[j][:, t, :], sl[:, bass.ds(r, 1), COL_GATE:COL_GATE + 1],
                                                          sl[:, bass.ds(r, 1), 0:D], ALU.mult, ALU.add)
                step.then_inc(y_ready[j], 1)

            def split_w1(n, j):
                dve.wait_ge(w1_high_ready, n + 1)
                for c in range(DC):
                    step = nc.vector.tensor_tensor(w1_low[j][:, c, :], w1_in_sb[:, c, :], w1_high[j][:, c, :].bitcast(f32), ALU.subtract)
                step.then_inc(w1_split, 1)

            def gathered_low(k, j):
                dve.wait_ge(gT_ready, 2 * k + j + 1)
                nc.vector.tensor_tensor(xg_low[j][:, :, :], ps_gT, xg_high[j][:, :, :].bitcast(f32), ALU.subtract).then_inc(xg_split, 1)

            def hidden_low(k, j):
                e = 2 * k + j
                for q in range(FC // 2):
                    dve.wait_ge(h_high_ready, (FC // 2) * e + q + 1)
                    nc.vector.scalar_tensor_tensor(h_low[j][:, 2 * q:2 * q + 2, :], ps_h[q], 0.0,
                                                   h_high[j][:, 2 * q:2 * q + 2, :].bitcast(f32), ALU.max, ALU.subtract).then_inc(h_split, 1)

            def expert(k, j, two_on=True):
                if two_on:
                    gathered(k + 1, j)
                hidden_low(*((k, 1) if j == 0 else (k + 1, 0)))
                if two_on:
                    gathered_low(k + 1, j)
                    split_w1(2 * k + j + 2, j)
                output_rows(k, j)

            peeled(0, batch, before_it=False)
            split_w1(0, 0)
            pairs(dve, 1, B - 2, batch)
            peeled(B - 1, batch, next_one=False)
            for part in (residual, normalised, choose, place_rows):
                peeled(B - 1, part)

            split_w1(1, 1)
            for n in range(2):
                peeled(n, gathered)
            for n in range(2):
                peeled(n, gathered_low)
            peeled(0, hidden_low)
            pairs(dve, 0, E - 3, expert)
            peeled(E - 2, expert, two_on=False)
            peeled(E - 1, output_rows)


_INS = ["x", "L0_conv_Wq", "L0_conv_bq", "L0_conv_Wk", "L0_conv_bk", "L0_conv_Wv", "L0_conv_bv", "L0_conv_Wo",
        "L0_conv_bo", "L0_conv_sigma", "L0_ffn_wg", "L0_ffn_w1", "L0_ffn_w2"]


def kernel(**inputs):
    import concourse.bacc as bacc
    from concourse.bass_utils import run_bass_kernel_spmd

    nc = bacc.Bacc("TRN2", target_bir_lowering=False, num_devices=1)
    arrays, args = {}, []
    table, ident, token = shape_constants()
    for name, a in [(n, inputs[n]) for n in _INS] + [("tables", table), ("eye", ident), ("tokens", token)]:
        a = np.ascontiguousarray(a)
        arrays[f"in_{name}"] = a
        args.append(nc.dram_tensor(f"in_{name}", a.shape, mybir.dt.from_np(a.dtype), kind="ExternalInput").ap())
    slots = nc.dram_tensor("slots", [N, RW], mybir.dt.float32, kind="Internal").ap()
    out = nc.dram_tensor("out_0", [B, HH, WW, D], mybir.dt.float32, kind="ExternalOutput").ap()
    build(nc, *args, slots, out)
    r = run_bass_kernel_spmd(nc, [arrays], core_ids=[0])
    return r.results[0]["out_0"]
```

```python
import numpy as np
from contextlib import ExitStack

import concourse.bass as bass
from concourse import mybir

B, HH, WW, D = 8, 16, 16, 256
TB = HH * WW
N = B * TB
P = 128
DC = D // P
NT = N // P
E, F = 8, 1024
CAP = N // E
FC = F // P
EPS_C, EPS_T = 1e-6, 1e-5
COL_TOK, COL_GATE, COL_NMR, COL_RSTD = D, D + 1, D + 2, D + 3
RW = D + 4
VW = D + E
MW = D + 2 * E
NOWHERE = 2 * N
X_GROUPS = ((0, 2), (2, 4), (4, 6), (6, 8), (8, 12), (12, NT))
WARM_UP, WARM_LAST, WARM_BETWEEN = 10, 4, 36
OFF = 1e30


def shape_constants():
    p = np.arange(P)
    k = np.arange(P)
    kk = np.arange(TB)
    same_row = (p[:, None] // WW) == (k[None, :] // WW)
    dist_row = np.where(same_row, (p[:, None] % WW - k[None, :] % WW) ** 2, 0)
    same_col = (p[:, None] % WW) == (kk[None, :] % WW)
    dist_col = [np.where(same_col, ((t * P + p[:, None]) // WW - kk[None, :] // WW) ** 2, 0) for t in range(TB // P)]
    upper = k[:, None] <= k[None, :]
    rank = np.tile(E - np.arange(E), (P, 2))
    off_row, off_col = np.where(same_row, 0, OFF), np.where(same_col, 0, OFF)
    table = np.concatenate([upper, dist_row, off_row, *dist_col, off_col, rank], 1).astype(np.float32)
    table = (table.view(np.uint32) >> 16).astype(np.uint16)
    ident = np.eye(P, dtype=np.float32)
    token = (np.arange(NT)[None, :] * P + p[:, None]).astype(np.int32)
    return np.ascontiguousarray(table), ident, np.ascontiguousarray(token)


TABLE_W = 3 * P + 3 * TB + 2 * E


def wait_apart(eng, sem, value, passed):
    wait(eng, sem, value)
    eng.sem_inc(passed, 1)


def wait(eng, sem, value):
    if isinstance(value, int) and value <= 0:
        return
    eng.wait_ge(sem, value)


class Chain:

    def __init__(self, eng, sem):
        self.eng, self.sem, self.n = eng, sem, 0

    def mark(self, instruction):
        instruction.then_inc(self.sem, 1)
        self.n += 1

    def done(self, instruction=None):
        if instruction is not None:
            self.mark(instruction)
        self.eng.wait_ge(self.sem, self.n)


def build(nc, x, Wq, bq, Wk, bk, Wv, bv, Wo, bo, sigma, wg, w1, w2, tables_in, eye, tokens, slots, out):
    f32, f32r, bf16, i32, u32 = mybir.dt.float32, mybir.dt.float32r, mybir.dt.bfloat16, mybir.dt.int32, mybir.dt.uint32
    ALU, ACT, AX = mybir.AluOpType, mybir.ActivationFunctionType, mybir.AxisListType

    ctx = ExitStack()
    with ctx:
        def sb(name, shape, dt=f32):
            return ctx.enter_context(nc.sbuf_tensor(name, shape, dt))

        def bank(name):
            return ctx.enter_context(nc.psum_tensor(name, [P, 512], f32))

        def sem(name):
            return ctx.enter_context(nc.semaphore(name))

        table_in = sb("table_in", [P, TABLE_W], mybir.dt.uint16)
        table = table_in[:, :].bitcast(bf16)
        upper, dist_row, off_row = (table[:, n * P:(n + 1) * P] for n in range(3))
        dist_col, off_col = table[:, 3 * P:3 * P + 2 * TB], table[:, 3 * P + 2 * TB:3 * P + 3 * TB]
        rank = table[:, 3 * P + 3 * TB:TABLE_W].rearrange("p (a b) -> p a b", a=2)
        ident_sb = sb("ident", [P, P])
        ident = ident_sb[:, :]
        token = sb("token", [P, NT], i32)
        ones = sb("ones", [P, P], bf16)
        w1_in_sb, w2_in_sb = sb("w1_in_sb", [P, DC, F]), sb("w2_in_sb", [P, FC, D])
        wq_sb, wk_sb, wv_sb, wo_sb = (w2_in_sb[:, DC * n:DC * (n + 1), :] for n in range(4))
        bq_sb, bv_sb, bo_cols = sb("bq_sb", [P, DC]), sb("bv_sb", [P, DC]), sb("bo_cols", [P, DC])
        bv_wide, bo_wide = sb("bv_wide", [P, DC, P]), sb("bo_wide", [P, DC, P])
        ones_wide = sb("ones_wide", [P, P])
        bo_sb = sb("bo_sb", [P, D])
        wg_sb = sb("wg_sb", [P, DC, E])
        sigma_sb = sb("sigma_sb", [P, 1])
        decay = sb("decay", [P, 2])
        mask_row, mask_col = sb("mask_row", [P, P]), sb("mask_col", [P, 2 * TB])
        a_high, a_low = (sb(f"a_{n}", [P, DC, D], f32r) for n in ("high", "low"))
        woT = sb("woT", [P, DC, VW])
        m_high, m_low = (sb(f"m_{n}", [P, DC, MW], f32r) for n in ("high", "low"))
        wgc = sb("wgc", [P, DC, E])
        ow = sb("ow", [P, E])
        qbias = sb("qbias", [P, DC])
        obias = sb("obias", [P, D])
        scrap = sb("scrap", [P, 1])
        minus_half = sb("minus_half", [P, NT])
        sl_sb = sb("sl", [P, NT * RW])
        sl = sl_sb[:, :].rearrange("p (t r) -> p t r", t=NT)
        x_sb = sl_sb[:, 0:NT * D].rearrange("p (t d) -> p t d", t=NT)
        stats = sb("stats", [P, NT, 6])
        mean_var = sb("mean_var", [P, NT, 2])
        var_eps, minus_mean, rstd, nmr, std = (sb(n, [P, NT]) for n in ("var_eps", "minus_mean", "rstd", "nmr", "std"))
        xn = sb("xn", [P, 2, D])
        xb = [sb(f"xb{j}", [P, 2, D]) for j in range(2)]
        xT_high, xT_low = ([sb(f"xT_{n}{j}", [P, DC, TB], f32r) for j in range(2)] for n in ("high", "low"))
        qT_high, qT_low = (sb(f"qT_{n}", [P, DC, TB], f32r) for n in ("high", "low"))
        v_sb = [sb(f"v_sb{j}", [P, 2, VW]) for j in range(2)]
        x_logit = sb("x_logit", [P, 2, E])
        pre_logit = [sb(f"pre_logit{j}", [P, 2, E]) for j in range(2)]
        s_row, s_col = sb("s_row", [P, 2, P]), sb("s_col", [P, 2, TB])
        ntop = sb("ntop", [P, 2, 2])
        e_row, e_col = sb("e_row", [P, 2, P]), sb("e_col", [P, 2, TB])
        esum, einv = sb("esum", [P, 4]), sb("einv", [P, 4])
        prob = sb("prob", [P, 2, TB])
        pT = sb("pT", [P, 2, TB])
        row = [sb(f"row{j}", [P, 2, RW]) for j in range(2)]
        row_last, slot_last = sb("row_last", [P, 2, RW]), sb("slot_last", [P, 2], i32)
        stats2, mean_var2 = sb("stats2", [P, 2, 6]), sb("mean_var2", [P, 2, 2])
        var_eps2 = sb("var_eps2", [P, 2])
        logit, lmax, shifted, lexp = sb("logit", [P, 2, E]), sb("lmax", [P, 2]), sb("shifted", [P, 2, E]), sb("lexp", [P, 2, E])
        ranked, rmax = sb("ranked", [P, 2, E]), sb("rmax", [P, 2])
        chosen = sb("chosen", [P, 2, E], bf16)
        both = sb("both", [P, E], bf16)
        before = [sb(f"before{j}", [P, E], bf16) for j in range(2)]
        gsum = sb("gsum", [P, 2])
        counted, loc, over, place_of = sb("counted", [P, 2, E]), sb("loc", [P, 2]), sb("over", [P, 2]), sb("place_of", [P, 2])
        slot = [sb(f"slot{j}", [P, 2], i32) for j in range(2)]
        empty = sb("empty", [P, RW])
        xs = [sb(f"xs{j}", [P, 2, D]) for j in range(2)]
        xg_high, xg_low = ([sb(f"xg_{n}{j}", [P, DC, CAP], f32r) for j in range(2)] for n in ("high", "low"))
        w1_high, w1_low = ([sb(f"w1_{n}{j}", [P, DC, F], f32r) for j in range(2)] for n in ("high", "low"))
        w2_high, w2_low = ([sb(f"w2_{n}{j}", [P, FC, D], f32r) for j in range(2)] for n in ("high", "low"))
        h_high, h_low = ([sb(f"h_{n}{j}", [P, FC, CAP], f32r) for j in range(2)] for n in ("high", "low"))
        y = [sb(f"y{j}", [P, 2, D]) for j in range(2)]
        goal = [sb(f"goal{j}", [P, 2], i32) for j in range(2)]

        def two_banks(name):
            return ctx.enter_context(nc.psum_tensor(name, [P, 2, 512], f32))

        def halves(a):
            return a.rearrange("p (a b) -> p a b", a=2)

        bank_xT, bank_q, bank_s, bank_pT = (bank(f"bank_{n}") for n in ("xT", "q", "s", "pT"))
        ps_xT, ps_q, ps_s, ps_pT = (halves(b[:, :]) for b in (bank_xT, bank_q, bank_s, bank_pT))
        ps_v, ps_o = two_banks("banks_v"), two_banks("banks_o")
        ps_count = bank_pT[:, 0:2 * E].rearrange("p (a b) -> p a b", a=2)
        ps_wgsum, ps_qbias, ps_obias, ps_ow = bank_pT[:, 0:E], bank_pT[:, E:E + DC], ps_o[:, 1, 0:D], ps_o[:, 1, D:VW]
        ps_wo_wgc = ps_o[:, 0, 0:DC * E].rearrange("p (a b) -> p a b", a=DC)
        ps_h = [ps_xT, ps_q, ps_s, halves(ps_v[:, 0, :])]
        ps_y = [halves(ps_v[:, 1, :]), ps_pT]
        ps_gT = [halves(ps_o[:, j, :]) for j in range(2)]
        ps_y_last = [ps_gT[0][:, 0, :], ps_y[1][:, 1, :]]

        const_in, eye_in, weights_in, wv_in, small_in, wg_in, token_in = (sem(n) for n in (
            "const_in", "eye_in", "weights_in", "wv_in", "small_in", "wg_in", "token_in"))
        bq_in, rows_in = sem("bq_in"), sem("rows_in")

        x_in = [sem(f"x_in{j}") for j in range(len(X_GROUPS))]
        w1_in, w2_in = sem("w1_in"), sem("w2_in")
        w1_high_ready, w1_split, w2_high_ready, w2_split = (sem(n) for n in ("w1_high_ready", "w1_split", "w2_high_ready", "w2_split"))
        row_free, y_free = sem("row_free"), sem("y_free")
        slots_in = [sem(f"slots_in{j}") for j in range(2)]
        x2_stored, x2_stored_last = [sem(f"x2_stored{j}") for j in range(2)], sem("x2_stored_last")
        row_sent, row_sent_last = [sem(f"row_sent{j}") for j in range(2)], sem("row_sent_last")
        y_sent = [sem(f"y_sent{j}") for j in range(2)]
        slots_empty, empty_ready = sem("slots_empty"), sem("empty_ready")
        ones_ready = sem("ones_ready")
        wide_ready = sem("wide_ready")
        setup_step = sem("setup_step")
        fold_a, fold_wo, fold_m = sem("fold_a"), sem("fold_wo"), sem("fold_m")
        qbias_made, wgsum_made, wo_wgc_made, obias_made = (sem(n) for n in ("qbias_made", "wgsum_made", "wo_wgc_made", "obias_made"))
        a_high_ready, a_ready, wo_ready, m_high_ready, m_ready, b_ready = (sem(n) for n in (
            "a_high_ready", "a_ready", "wo_ready", "m_high_ready", "m_ready", "b_ready"))
        wgc_ready, wo_wgc_ready, qbias_ready = sem("wgc_ready"), sem("wo_wgc_ready"), sem("qbias_ready")
        var_ready, rstd_ready, nmr_ready, std_ready = (sem(n) for n in ("var_ready", "rstd_ready", "nmr_ready", "std_ready"))
        xn_ready, xb_ready = sem("xn_ready"), sem("xb_ready")
        xT_made, xT_high_ready, xT_ready = sem("xT_made"), sem("xT_high_ready"), sem("xT_ready")
        q_made, q_high_ready, q_ready = sem("q_made"), sem("q_high_ready"), sem("q_ready")
        s_made, top_ready = sem("s_made"), sem("top_ready")
        v_made, v_ready, pre_ready = sem("v_made"), sem("v_ready"), sem("pre_ready")
        x_logit_ready = sem("x_logit_ready")
        e_ready, prob_ready = sem("e_ready"), sem("prob_ready")
        pT_made, pT_ready = sem("pT_made"), sem("pT_ready")
        o_made, x2_ready = sem("o_made"), sem("x2_ready")
        o_first_made = sem("o_first_made")
        var2_ready, rstd2_ready = sem("var2_ready"), sem("rstd2_ready")
        shifted_ready, lexp_ready = sem("shifted_ready"), sem("lexp_ready")
        chosen_ready, count_made, count_read, slot_ready = (sem(n) for n in ("chosen_ready", "count_made", "count_read", "slot_ready"))
        token_ready = sem("token_ready")
        attn_step, norm_step, place_step = sem("attn_step"), sem("norm_step"), sem("place_step")
        xs_ready, gT_made, gT_ready = sem("xs_ready"), sem("gT_made"), sem("gT_ready")
        xg_split, h_made, h_high_ready, h_split = sem("xg_split"), sem("h_made"), sem("h_high_ready"), sem("h_split")
        y_made, y_ready = sem("y_made"), [sem(f"y_ready{j}") for j in range(2)]
        goal_ready = sem("goal_ready")

        pool_passed, dve_passed = sem("pool_passed"), sem("dve_passed")
        block = ctx.enter_context(nc.Block())
        x_view = x.rearrange("b h w d -> (b h w) d").rearrange("(t p) d -> p t d", p=P)
        out_rows = out.rearrange("b h w d -> (b h w) d")
        out_view = out_rows.rearrange("(t p) d -> p t d", p=P)
        slots_view = slots.rearrange("(t p) r -> p t r", p=P)
        w1_view = w1.rearrange("e (c p) f -> e p c f", p=P)
        w2_view = w2.rearrange("e (c p) d -> e p c d", p=P)

        def matrix(w):
            return w.rearrange("(c p) d -> p c d", p=P)

        def pairs(eng, first, last, body):
            assert (last - first) % 2 == 1
            with eng.Fori(0, (last - first + 1) // 2) as turn:
                for step in range(2):
                    n = first + step
                    body(turn + n // 2, n % 2)

        def peeled(n, body, **how):
            body(n // 2, n % 2, **how)

        def after(k, j):
            return (k, 1) if j == 0 else (k + 1, 0)

        def row_of(k, j):
            return row_last if isinstance(k, int) and 2 * k + j == B - 1 else row[j]

        def slot_of(k, j):
            return slot_last if row_of(k, j) is row_last else slot[j]

        def sweep(eng, body):
            peeled(0, body, first=True, second=True)
            peeled(1, body, second=True)
            pairs(eng, 2, B - 3, body)
            peeled(B - 2, body, last_but_one=True)
            peeled(B - 1, body, last_but_one=True, last=True)

        @block.sync
        def _(sp):
            def load_x(g):
                a, b = X_GROUPS[g]
                sp.dma_start(x_sb[:, a:b, :], x_view[:, a:b, :]).then_inc(x_in[g], 16)

            sp.dma_start(wk_sb, matrix(Wk)).then_inc(weights_in, 16)
            load_x(0)
            load_x(1)
            with nc.allow_non_contiguous_dma(reason="bias columns of 128"):
                sp.dma_start(bq_sb[:, :], bq.rearrange("(c p) -> p c", p=P)).then_inc(bq_in, 16)
                sp.dma_start(wg_sb[:, :, :], wg.rearrange("(c p) e -> p c e", p=P)).then_inc(wg_in, 16)
                sp.dma_start(wv_sb, matrix(Wv)).then_inc(wv_in, 16)
                for columns, b in ((bv_sb, bv), (bo_cols, bo)):
                    sp.dma_start(columns[:, :], b.rearrange("(c p) -> p c", p=P)).then_inc(small_in, 16)
            sp.dma_start(table_in[:, :], tables_in).then_inc(const_in, 16)
            load_x(2)
            sp.dma_start(w1_in_sb[:, :, :], w1_view[0]).then_inc(w1_in, 16)
            for g in range(3, len(X_GROUPS)):
                load_x(g)
            sp.dma_start(token[:, :], tokens).then_inc(token_in, 16)
            sp.sem_inc(row_free, 4)
            sp.wait_ge(xT_made, 1)
            sp.wait_ge(empty_ready, 1)
            sp.dma_start(slots_view, empty[:, None, :].to_broadcast([P, NT, RW])).then_inc(slots_empty, 16)
            sp.wait_ge(m_ready, 1)
            sp.dma_start(w2_in_sb[:, :, :], w2_view[0]).then_inc(w2_in, 16)

            def store_x2(k, j):
                sp.wait_ge(x2_ready, 2 * k + j + 1)
                sp.dma_start(out_view[:, bass.ds(4 * k + 2 * j, 2), :], row[j][:, :, 0:D]).then_inc(x2_stored[j], 16)
                sp.wait_ge(x2_stored[j], 16 * (k + 1))
                sp.sem_inc(row_free, 1)
                sp.wait_ge(row_sent[j], 32 * (k + 1))
                sp.sem_inc(row_free, 1)

            peeled(0, store_x2)
            sp.wait_ge(w1_split, 1)
            sp.dma_start(w1_in_sb[:, :, :], w1_view[1]).then_inc(w1_in, 16)
            pairs(sp, 1, B - 2, store_x2)
            sp.wait_ge(row_sent_last, 32)

            def load_slots(k, j):
                wait(sp, slots_in[j], 16 * k)
                sp.dma_start(sl[:, bass.ds(4 * k + 2 * j, 2), :], slots_view[:, bass.ds(4 * k + 2 * j, 2), :]).then_inc(slots_in[j], 16)

            peeled(0, load_slots)
            peeled(1, load_slots)
            sp.wait_ge(w1_split, 2)
            sp.dma_start(w1_in_sb[:, :, :], w1_view[2]).then_inc(w1_in, 16)
            sp.wait_ge(w2_split, 1)
            sp.dma_start(w2_in_sb[:, :, :], w2_view[1]).then_inc(w2_in, 16)
            pairs(sp, 2, E - 1, load_slots)
            sp.sem_inc(y_free, 2)

            def load_weights(k, j, w1_too=True):
                e = 2 * k + j
                sp.wait_ge(w2_split, e)
                sp.dma_start(w2_in_sb[:, :, :], w2_view[e]).then_inc(w2_in, 16)
                if w1_too:
                    sp.wait_ge(w1_split, e + 1)
                    sp.dma_start(w1_in_sb[:, :, :], w1_view[e + 1]).then_inc(w1_in, 16)
                sp.wait_ge(y_sent[j], 32 * k)
                sp.sem_inc(y_free, 1)

            pairs(sp, 2, E - 3, load_weights)
            peeled(E - 2, load_weights)
            peeled(E - 1, load_weights, w1_too=False)
            for j in range(2):
                sp.wait_ge(y_sent[j], 32 * (E // 2))

        @block.gpsimd
        def _(pool):
            nc.gpsimd.memset(empty[:, :], 0.0).then_inc(token_ready, 1)
            pool.wait_ge(token_ready, 1)
            nc.gpsimd.memset(empty[:, COL_TOK:COL_TOK + 1].bitcast(i32), NOWHERE).then_inc(empty_ready, 1)
            nc.gpsimd.dma_start(sigma_sb[:, :], sigma[None, :].to_broadcast([P, 1])).then_inc(rows_in, 16)
            nc.gpsimd.dma_start(bo_sb[:, :], bo[None, :].to_broadcast([P, D])).then_inc(rows_in, 16)
            def first_rstd(g):
                a, b = X_GROUPS[g]
                pool.wait_ge(var_ready, g + 1)
                nc.gpsimd.tensor_tensor(rstd[:, a:b], var_eps[:, a:b], minus_half[:, a:b], ALU.pow).then_inc(rstd_ready, 1)
                pool.wait_ge(rstd_ready, g + 1)
                nc.gpsimd.tensor_tensor(nmr[:, a:b], minus_mean[:, a:b], rstd[:, a:b], ALU.mult).then_inc(nmr_ready, 1)
                nc.gpsimd.tensor_tensor(std[:, a:b], var_eps[:, a:b], rstd[:, a:b], ALU.mult).then_inc(std_ready, 1)

            for g in range(2):
                first_rstd(g)
            pool.wait_ge(ones_ready, 1)
            pool.wait_ge(small_in, 32)
            bv_cols_wide, bo_cols_wide = (b[:, :].unsqueeze(2).to_broadcast([P, DC, P]) for b in (bv_sb, bo_cols))
            nc.gpsimd.tensor_tensor(bv_wide[:, :, :], bv_cols_wide, bv_cols_wide, ALU.add)
            nc.gpsimd.tensor_tensor(bo_wide[:, :, :], bo_cols_wide, ones_wide[:, :].unsqueeze(1).to_broadcast([P, DC, P]),
                                    ALU.mult).then_inc(wide_ready, 1)
            first_rstd(2)
            first_rstd(3)
            pool.wait_ge(w1_high_ready, DC)
            nc.gpsimd.tensor_tensor(w1_low[0][:, :, :], w1_in_sb[:, :, :], w1_high[0][:, :, :].bitcast(f32), ALU.subtract).then_inc(w1_split, 1)
            first_rstd(4)
            pool.wait_ge(b_ready, 1)

            def rstd2(k, j):
                pool.wait_ge(var2_ready, 2 * k + j + 1)
                nc.gpsimd.tensor_tensor(row_of(k, j)[:, :, COL_RSTD], var_eps2[:, :], minus_half[:, 0:2], ALU.pow).then_inc(rstd2_ready, 1)

            def scatter_rows(k, j, tiles=range(2)):
                if 0 in tiles:
                    wait_apart(pool, slot_ready, 2 * k + j + 1, pool_passed)
                for t in tiles:
                    nc.gpsimd.indirect_dma_start(
                        slots, bass.IndirectOffsetOnAxis(ap=slot_of(k, j)[:, t:t + 1].bitcast(u32), axis=0),
                        row_of(k, j)[:, t, :], None, bounds_check=N - 1, oob_is_err=False).then_inc(
                            row_sent_last if row_of(k, j) is row_last else row_sent[j], 16)

            def batch(k, j, first=False, second=False, last_but_one=False, last=False):
                if last:
                    pool.wait_ge(x2_ready, B - 2)
                elif not second:
                    rstd2(k - 1, j)
                nc.gpsimd.tensor_tensor(xb[j][:, :, :], x_sb[:, bass.ds(4 * k + 2 * j, 2), :],
                                        obias[:, None, :].to_broadcast([P, 2, D]), ALU.add).then_inc(xb_ready, 1)
                if last:
                    rstd2(k - 1, j)
                if second and not first:
                    first_rstd(5)
                pool.wait_ge(x_logit_ready, 2 * k + j + 1)
                nc.gpsimd.tensor_tensor(pre_logit[j][:, :, :], x_logit[:, :, :], ow[:, None, :].to_broadcast([P, 2, E]), ALU.add).then_inc(pre_ready, 1)
                if not second:
                    scatter_rows(k - 1, j)
                elif not first:
                    pool.wait_ge(slots_empty, 16)

            def split_w2(n, j):
                for part in range(2):
                    pool.wait_ge(w2_high_ready, 2 * n + part + 1)
                    half = slice(part * FC // 2, (part + 1) * FC // 2)
                    step = nc.gpsimd.tensor_tensor(w2_low[j][:, half, :], w2_in_sb[:, half, :], w2_high[j][:, half, :].bitcast(f32), ALU.subtract)
                step.then_inc(w2_split, 1)

            sweep(pool, batch)
            peeled(B - 2, rstd2)
            peeled(B - 2, scatter_rows, tiles=[0])
            peeled(B - 1, rstd2)
            peeled(B - 2, scatter_rows, tiles=[1])
            peeled(B - 1, scatter_rows)
            split_w2(0, 0)

            for j in range(2):
                pool.wait_ge(x2_stored[j], 16 * (B // 2 - j))
            pool.wait_ge(x2_stored_last, 16)

            def scatter_y(k, j, last=False):
                pool.wait_ge(goal_ready, 2 * k + j + 1)
                for c in range(2):
                    if last or c == 0:
                        wait_apart(pool, y_ready[j], k + 1 + c, pool_passed)
                    nc.gpsimd.indirect_dma_start(
                        out_rows, bass.IndirectOffsetOnAxis(ap=goal[j][:, c:c + 1].bitcast(u32), axis=0),
                        y[j][:, c, :], None, bounds_check=N - 1, oob_is_err=False).then_inc(y_sent[j], 16)

            def expert(k, j):
                split_w2(2 * k + j + 1, 1 - j)
                scatter_y(k, j)

            pairs(pool, 0, E - 3, expert)
            peeled(E - 2, expert)
            peeled(E - 1, scatter_y, last=True)

        @block.tensor
        def _(pe):
            def product(out_ap, lhs, rhs, columns, rows):
                for c in range(DC):
                    step = nc.tensor.matmul(out_ap, lhs[:, c, columns], rhs[:, c, rows], start=c == 0, stop=c == DC - 1)
                return step

            def three_passes(out_ap, stationary, moving, last="moving", before_last=None):
                n = len(stationary)
                for c in range(n):
                    (a_h, a_l), (b_h, b_l) = stationary[c], moving[c]
                    second = (a_h, b_l) if last == "stationary" else (a_l, b_h)
                    nc.tensor.matmul(out_ap, a_h, b_h, start=c == 0, stop=False)
                    nc.tensor.matmul(out_ap, *second, start=False, stop=False)
                if before_last:
                    before_last()
                for c in range(n):
                    (a_h, a_l), (b_h, b_l) = stationary[c], moving[c]
                    third = (a_l, b_h) if last == "stationary" else (a_h, b_l)
                    step = nc.tensor.matmul(out_ap, *third, start=False, stop=c == n - 1)
                return step

            chunk = [slice(d * P, (d + 1) * P) for d in range(DC)]
            whole = slice(0, None)

            def transpose_x(k, j):
                i = 2 * k + j
                pe.wait_ge(xn_ready, i + 1)
                wait(pe, xT_ready, i)
                for t in range(2):
                    for c in range(DC):
                        step = nc.tensor.transpose(ps_xT[:, c, t * P:(t + 1) * P], xn[:, t, c * P:(c + 1) * P], ident)
                step.then_inc(xT_made, 1)

            def query(k, j):
                i = 2 * k + j
                pe.wait_ge(xT_high_ready, i + 1)
                wait(pe, q_ready, i)
                for d in range(DC):
                    step = three_passes(ps_q[:, d, :], [(a_high[:, c, chunk[d]], a_low[:, c, chunk[d]]) for c in range(DC)],
                                        [(xT_high[j][:, c, :], xT_low[j][:, c, :]) for c in range(DC)],
                                        before_last=(lambda: pe.wait_ge(xT_ready, i + 1)) if d == 0 else None)
                step.then_inc(q_made, 1)

            def scores(k, j):
                i = 2 * k + j
                pe.wait_ge(q_high_ready, i + 1)
                wait(pe, top_ready, 4 * i)
                for t in range(2):
                    step = three_passes(ps_s[:, t, :], [(qT_high[:, c, chunk[t]], qT_low[:, c, chunk[t]]) for c in range(DC)],
                                        [(xT_high[j][:, c, :], xT_low[j][:, c, :]) for c in range(DC)], last="stationary",
                                        before_last=(lambda: pe.wait_ge(q_ready, i + 1)) if t == 0 else None)
                step.then_inc(s_made, 1)

            def values(k, j):
                i = 2 * k + j
                wait(pe, x_logit_ready, i)
                for t in range(2):
                    step = three_passes(ps_v[:, t, 0:MW], [(xT_high[j][:, c, chunk[t]], xT_low[j][:, c, chunk[t]]) for c in range(DC)],
                                        [(m_high[:, c, :], m_low[:, c, :]) for c in range(DC)])
                step.then_inc(v_made, 1)

            def transpose_prob(k, j):
                i = 2 * k + j
                pe.wait_ge(prob_ready, i + 1)
                wait(pe, pT_ready, i)
                pe.wait_ge(count_read, i + 1)
                for t in range(2):
                    for c in range(2):
                        step = nc.tensor.transpose(ps_pT[:, c, t * P:(t + 1) * P], prob[:, t, c * P:(c + 1) * P], ident)
                step.then_inc(pT_made, 1)

            def attention_out(k, j, t):
                i = 2 * k + j
                if t == 0:
                    pe.wait_ge(pT_ready, i + 1)
                    pe.wait_ge(v_ready, i + 1)
                    wait(pe, x2_ready, i)
                    wait(pe, norm_step, 9 * (i - 1) + 1)
                for c in range(2):
                    step = nc.tensor.matmul(ps_o[:, t, 0:VW], pT[:, c, t * P:(t + 1) * P], v_sb[j][:, c, :], start=c == 0, stop=c == 1)
                if t == 1:
                    step.then_inc(o_made, 1)
                elif isinstance(k, int) and i == B - 1:
                    step.then_inc(o_first_made, 1)

            def counts(k, j):
                pe.wait_ge(chosen_ready, 2 * k + j + 1)
                nc.tensor.matmul(ps_count[:, 0, :], upper, chosen[:, 0, :], start=True, stop=False)
                nc.tensor.matmul(ps_count[:, 0, :], ones[:, :], before[j][:, :], start=False, stop=True)
                nc.tensor.matmul(ps_count[:, 1, :], upper, chosen[:, 1, :], start=True, stop=False)
                nc.tensor.matmul(ps_count[:, 1, :], ones[:, :], chosen[:, 0, :], start=False, stop=False)
                nc.tensor.matmul(ps_count[:, 1, :], ones[:, :], before[j][:, :], start=False, stop=True).then_inc(count_made, 1)

            def batch(k, j, first=False, second=False, last_but_one=False, last=False):
                if not last:
                    transpose_x(*after(k, j))
                scores(k, j)
                previous = (k, 0) if j == 1 else (k - 1, 1)
                if not first:
                    transpose_prob(*previous)
                if first:
                    fold_biases()
                    query(*after(k, j))
                    pe.wait_ge(m_ready, 1)
                values(k, j)
                if not last and not first:
                    query(*after(k, j))
                if not first:
                    attention_out(*previous, 0)
                if not second:
                    counts(k - 1, j)
                if not first:
                    attention_out(*previous, 1)

            def fold_logits():
                for d in range(DC):
                    step = product(ps_wo_wgc[:, d, :], wo_sb, wgc, chunk[d], whole)
                step.then_inc(wo_wgc_made, 1)

            def fold_values():
                pe.wait_ge(wo_ready, 1)
                pe.wait_ge(wo_wgc_ready, 1)
                pe.wait_ge(wv_in, 16)
                for d in range(DC):
                    step = product(ps_v[:, d, 0:VW], wv_sb, woT, chunk[d], whole)
                step.then_inc(fold_m, 1)

            def fold_biases():
                pe.wait_ge(wide_ready, 1)
                for c in range(DC):
                    nc.tensor.matmul(ps_o[:, 1, 0:VW], bv_wide[:, c, :], woT[:, c, :], start=c == 0, stop=False)
                for c in range(DC):
                    step = nc.tensor.matmul(ps_ow, bo_wide[:, c, :], wgc[:, c, :], start=False, stop=c == DC - 1)
                step.then_inc(obias_made, 1)

            def keep_warm(n):
                for _ in range(n):
                    nc.tensor.matmul(ps_xT[:, 0, 0:P], ones_wide[:, :], ones_wide[:, :], start=True, stop=True)

            pe.wait_ge(ones_ready, 1)
            keep_warm(WARM_UP)
            pe.wait_ge(weights_in, 32)
            for d in range(DC):
                step = product(ps_q[:, d, :], wq_sb, wk_sb, chunk[d], whole)
            step.then_inc(fold_a, 1)
            pe.wait_ge(wg_in, 16)
            for c in range(DC):
                step = nc.tensor.matmul(ps_wgsum, ones_wide[:, :], wg_sb[:, c, :], start=c == 0, stop=c == DC - 1)
            step.then_inc(wgsum_made, 1)
            pe.wait_ge(eye_in, 32)
            peeled(0, transpose_x)
            for c in range(DC):
                for m in range(DC):
                    step = nc.tensor.transpose(ps_s[:, m, c * P:(c + 1) * P], wo_sb[:, c, m * P:(m + 1) * P], ident)
            step.then_inc(fold_wo, 1)
            pe.wait_ge(bq_in, 16)
            pe.wait_ge(wgc_ready, 1)
            for d in range(DC):
                step = product(ps_qbias[:, d:d + 1], wk_sb, bq_sb[:, :].unsqueeze(2), chunk[d], whole)
            step.then_inc(qbias_made, 1)
            fold_logits()
            pe.wait_ge(a_ready, 1)
            peeled(0, query)
            fold_values()
            sweep(pe, batch)
            peeled(B - 1, transpose_prob)
            keep_warm(WARM_LAST)
            peeled(B - 1, attention_out, t=0)
            peeled(B - 2, counts)
            peeled(B - 1, attention_out, t=1)
            peeled(B - 1, counts)

            def gather_T(k, j):
                e = 2 * k + j
                pe.wait_ge(xs_ready, e + 1)
                for t in range(2):
                    for c in range(DC):
                        step = nc.tensor.transpose(ps_gT[j][:, c, t * P:(t + 1) * P], xs[j][:, t, c * P:(c + 1) * P], ident)
                step.then_inc(gT_made, 1)

            def hidden(k, j):
                e = 2 * k + j
                pe.wait_ge(w1_split, e + 1)
                pe.wait_ge(gT_ready, e + 1)
                for q in range(FC // 2):
                    wait(pe, h_split, (FC // 2) * (e - 1) + q + 1)
                    for u in range(2):
                        f = slice((2 * q + u) * P, (2 * q + u + 1) * P)
                        step = three_passes(ps_h[q][:, u, :], [(w1_high[j][:, c, f], w1_low[j][:, c, f]) for c in range(DC)],
                                            [(xg_high[j][:, c, :], xg_low[j][:, c, :]) for c in range(DC)],
                                            before_last=(lambda: pe.wait_ge(xg_split, e + 1)) if q == u == 0 else None)
                    step.then_inc(h_made, 1)

            def expert_out(k, j, last=False):
                e = 2 * k + j
                pe.wait_ge(w2_split, e + 1)
                pe.wait_ge(h_split, (FC // 2) * (e + 1))
                for t in range(2):
                    own = slice(t * P, (t + 1) * P)
                    step = three_passes(ps_y_last[t] if last else ps_y[j][:, t, :],
                                        [(h_high[j][:, f, own], h_low[j][:, f, own]) for f in range(FC)],
                                        [(w2_high[j][:, f, :], w2_low[j][:, f, :]) for f in range(FC)])
                    if last or t == 1:
                        step.then_inc(y_made, 1)

            def expert(k, j, two_on=True):
                hidden(*((k, 1) if j == 0 else (k + 1, 0)))
                if two_on:
                    gather_T(k + 1, j)
                expert_out(k, j)

            keep_warm(WARM_BETWEEN)
            peeled(0, gather_T)
            peeled(1, gather_T)
            peeled(0, hidden)
            pairs(pe, 0, E - 3, expert)
            peeled(E - 2, expert, two_on=False)
            pe.wait_ge(y_ready[1], E // 2 - 1)
            peeled(E - 1, expert_out, last=True)

        @block.scalar
        def _(act):
            act.dma_start(wq_sb, matrix(Wq)).then_inc(weights_in, 16)
            act.dma_start(wo_sb, matrix(Wo)).then_inc(eye_in, 16)
            act.dma_start(ident_sb[:, :], eye).then_inc(eye_in, 16)

            def normalised_x(k, j):
                i = 2 * k + j
                wait(act, xT_made, i)
                for t in range(2):
                    r = 4 * k + 2 * j + t
                    step = nc.scalar.activation(xn[:, t, :], x_sb[:, bass.ds(r, 1), :], ACT.Identity,
                                                scale=rstd[:, bass.ds(r, 1)], bias=nmr[:, bass.ds(r, 1)])
                step.then_inc(xn_ready, 1)

            act.wait_ge(ones_ready, 1)
            nc.scalar.activation(scrap[:, :], ones_wide[:, 0:1], ACT.Exp)
            act.wait_ge(nmr_ready, 1)
            peeled(0, normalised_x)

            def transposed_x(k, j):
                act.wait_ge(xT_made, 2 * k + j + 1)
                nc.scalar.activation(xT_high[j][:, :, :], ps_xT, ACT.Copy).then_inc(xT_high_ready, 1)

            def query(k, j):
                i = 2 * k + j
                act.wait_ge(q_made, i + 1)
                for d in range(DC):
                    step = nc.scalar.activation(qT_high[:, d, :], ps_q[:, d, :], ACT.Identity, bias=qbias[:, d:d + 1])
                step.then_inc(q_high_ready, 1)

            def transposed_prob(k, j):
                act.wait_ge(pT_made, 2 * k + j + 1)
                wait(act, o_made, 2 * k + j)
                nc.scalar.activation(pT[:, :, :], ps_pT, ACT.Copy).then_inc(pT_ready, 1)

            def exponentials(k, j):
                for t in range(2):
                    act.wait_ge(top_ready, 4 * (2 * k + j) + 2 * t + 2)
                    nc.scalar.activation(e_col[:, t, :], s_col[:, t, :], ACT.Exp, bias=ntop[:, t, 0:1], scale=-1.0, accum_out=esum[:, t:t + 1])
                    step = nc.scalar.activation(e_row[:, t, :], s_row[:, t, :], ACT.Exp, bias=ntop[:, t, 1:2], scale=-1.0, accum_out=esum[:, 2 + t:3 + t])
                step.then_inc(e_ready, 1)

            def values(k, j):
                act.wait_ge(v_made, 2 * k + j + 1)
                wait(act, pre_ready, 2 * k + j)
                nc.scalar.activation(v_sb[j][:, :, :], ps_v[:, :, 0:VW], ACT.Copy).then_inc(v_ready, 1)
                for t in range(2):
                    step = nc.scalar.activation(x_logit[:, t, :], ps_v[:, t, VW:MW], ACT.Copy, scale=std[:, bass.ds(4 * k + 2 * j + t, 1)])
                step.then_inc(x_logit_ready, 1)

            def gate_exp(k, j):
                i = 2 * k + j
                act.wait_ge(shifted_ready, i + 1)
                act.wait_ge(rstd2_ready, i + 1)
                for t in range(2):
                    step = nc.scalar.activation(lexp[:, t, :], shifted[:, t, :], ACT.Exp, scale=row_of(k, j)[:, t, COL_RSTD:COL_RSTD + 1],
                                                accum_out=gsum[:, t:t + 1])
                step.then_inc(lexp_ready, 1)

            def batch(k, j, first=False, second=False, last_but_one=False, last=False):
                if not last:
                    transposed_x(*after(k, j))
                if not last_but_one and not first:
                    act.wait_ge(nmr_ready, 4 if second else len(X_GROUPS))
                    normalised_x(k + 1, j)
                if first:
                    values_high()
                else:
                    transposed_prob(*((k, 0) if j == 1 else (k - 1, 1)))
                exponentials(k, j)
                if not last:
                    query(*after(k, j))
                if first:
                    act.wait_ge(nmr_ready, 3)
                    normalised_x(k + 1, j)
                values(k, j)
                if not second:
                    gate_exp(k - 1, j)

            def split_w(high, loaded, raw, ready, n, j):
                act.wait_ge(loaded, 16 * (n + 1))
                parts = raw.shape[1] // 2
                for part in range(2):
                    half = slice(part * parts, (part + 1) * parts)
                    nc.scalar.activation(high[j][:, half, :], raw[:, half, :], ACT.Copy).then_inc(ready, 1)

            def split_w1(n, j):
                split_w(w1_high, w1_in, w1_in_sb, w1_high_ready, n, j)

            def split_w2(n, j):
                split_w(w2_high, w2_in, w2_in_sb, w2_high_ready, n, j)

            act.wait_ge(fold_a, 1)
            nc.scalar.activation(a_high[:, :, :], ps_q, ACT.Copy, scale=-1.0).then_inc(a_high_ready, 1)
            peeled(0, transposed_x)
            act.wait_ge(fold_wo, 1)
            nc.scalar.activation(woT[:, :, 0:D], ps_s, ACT.Copy).then_inc(wo_ready, 1)
            act.wait_ge(nmr_ready, 2)
            peeled(1, normalised_x)
            act.wait_ge(qbias_ready, 1)
            peeled(0, query)

            def values_high():
                act.wait_ge(wgc_ready, 1)
                nc.scalar.activation(m_high[:, :, VW:MW], wgc[:, :, :], ACT.Copy)
                act.wait_ge(fold_m, 1)
                nc.scalar.activation(m_high[:, :, 0:VW], ps_v[:, :, 0:VW], ACT.Copy).then_inc(m_high_ready, 1)

            split_w1(0, 0)
            sweep(act, batch)
            peeled(B - 1, transposed_prob)
            peeled(B - 2, gate_exp)
            act.wait_ge(x2_ready, B)
            act.dma_start(out_view[:, NT - 2:NT, :], row_last[:, :, 0:D]).then_inc(x2_stored_last, 16)
            peeled(B - 1, gate_exp)
            split_w2(0, 0)

            def gathered_T(k, j):
                act.wait_ge(gT_made, 2 * k + j + 1)
                nc.scalar.activation(xg_high[j][:, :, :], ps_gT[j], ACT.Copy).then_inc(gT_ready, 1)

            def hidden(k, j, w2_next=None):
                e = 2 * k + j
                for q in range(FC // 2):
                    act.wait_ge(h_made, (FC // 2) * e + q + 1)
                    nc.scalar.activation(h_high[j][:, 2 * q:2 * q + 2, :], ps_h[q], ACT.Relu).then_inc(h_high_ready, 1)
                    if q == 1 and w2_next:
                        split_w2(*w2_next)

            def expert(k, j, two_on=True):
                e = 2 * k + j
                hidden(*((k, 1) if j == 0 else (k + 1, 0)), w2_next=(e + 1, 1 - j))
                if two_on:
                    gathered_T(k + 1, j)
                    split_w1(e + 2, j)

            split_w1(1, 1)
            peeled(0, gathered_T)
            peeled(1, gathered_T)
            peeled(0, hidden)
            pairs(act, 0, E - 3, expert)
            peeled(E - 2, expert, two_on=False)

        @block.vector
        def _(dve):
            setup = Chain(dve, setup_step)
            nc.vector.memset(ones_wide[:, :], 1.0).then_inc(ones_ready, 1)
            dve.sem_inc(count_read, 2)
            nc.vector.memset(minus_half[:, :], -0.5)
            nc.vector.memset(before[0][:, :], 0.0)
            setup.mark(nc.vector.memset(ones[:, :], 1.0))

            def first_norm(g):
                a, b = X_GROUPS[g]
                dve.wait_ge(x_in[g], 16)
                for i in range(a, b):
                    setup.mark(nc.vector.bn_stats(stats[:, i, :], x_sb[:, i, :]))
                setup.done()
                for i in range(a, b):
                    setup.mark(nc.vector.bn_aggr(mean_var[:, i, :], stats[:, i, :]))
                setup.done()
                nc.vector.tensor_scalar(minus_mean[:, a:b], mean_var[:, a:b, 0], -1.0, None, ALU.mult)
                nc.vector.tensor_scalar(var_eps[:, a:b], mean_var[:, a:b, 1], EPS_C, None, ALU.add).then_inc(var_ready, 1)

            def low_part(low, exact, high):
                return nc.vector.tensor_tensor(low, exact, high.bitcast(f32), ALU.subtract)

            def x_low(k, j):
                dve.wait_ge(xT_high_ready, 2 * k + j + 1)
                low_part(xT_low[j][:, :, :], ps_xT, xT_high[j][:, :, :]).then_inc(xT_ready, 1)

            def query_low(k, j):
                dve.wait_ge(q_high_ready, 2 * k + j + 1)
                for d in range(DC):
                    step = nc.vector.scalar_tensor_tensor(qT_low[:, d, :], ps_q[:, d, :], qbias[:, d:d + 1],
                                                          qT_high[:, d, :].bitcast(f32), ALU.add, ALU.subtract)
                step.then_inc(q_ready, 1)

            def masks():
                dve.wait_ge(const_in, 16)
                dve.wait_ge(rows_in, 32)
                setup.mark(nc.vector.tensor_tensor(decay[:, 0:1], sigma_sb[:, :], sigma_sb[:, :], ALU.mult))
                setup.done()
                setup.done(nc.vector.reciprocal(decay[:, 1:2], decay[:, 0:1]))
                setup.done(nc.vector.tensor_scalar(decay[:, 0:1], decay[:, 1:2], 0.5, None, ALU.mult))
                setup.mark(nc.vector.scalar_tensor_tensor(mask_row[:, :], dist_row, decay[:, 0:1], off_row, ALU.mult, ALU.add))
                setup.mark(nc.vector.scalar_tensor_tensor(halves(mask_col[:, :]), halves(dist_col), decay[:, 0:1],
                                                          off_col.unsqueeze(1).to_broadcast([P, 2, TB]), ALU.mult, ALU.add))

            first_norm(0)
            first_norm(1)
            dve.wait_ge(wgsum_made, 1)
            setup.done(nc.vector.scalar_tensor_tensor(wgc[:, :, :], ps_wgsum.unsqueeze(1).to_broadcast([P, DC, E]), -1.0 / D,
                                                      wg_sb[:, :, :], ALU.mult, ALU.add))
            dve.sem_inc(wgc_ready, 1)
            dve.wait_ge(a_high_ready, 1)
            nc.vector.scalar_tensor_tensor(a_low[:, :, :], ps_q, -1.0, a_high[:, :, :].bitcast(f32), ALU.mult, ALU.subtract).then_inc(a_ready, 1)
            peeled(0, x_low)
            dve.wait_ge(qbias_made, 1)
            nc.vector.tensor_scalar(qbias[:, :], ps_qbias, -1.0, None, ALU.mult).then_inc(qbias_ready, 1)
            dve.wait_ge(wo_wgc_made, 1)
            nc.vector.tensor_copy(woT[:, :, D:VW], ps_wo_wgc).then_inc(wo_wgc_ready, 1)
            masks()
            first_norm(2)
            peeled(0, query_low)
            first_norm(3)

            def values_low():
                dve.wait_ge(m_high_ready, 1)
                low_part(m_low[:, :, VW:MW], wgc[:, :, :], m_high[:, :, VW:MW])
                low_part(m_low[:, :, 0:VW], ps_v[:, :, 0:VW], m_high[:, :, 0:VW]).then_inc(m_ready, 1)

            setup.done()

            def bias_rows():
                dve.wait_ge(obias_made, 1)
                setup.mark(nc.vector.tensor_copy(ow[:, :], ps_ow))
                nc.vector.tensor_tensor(obias[:, :], ps_obias, bo_sb[:, :], ALU.add).then_inc(b_ready, 1)

            def maxima(k, j):
                def column(t):
                    nc.vector.tensor_tensor_reduce(
                        out=s_col[:, t, :], in0=ps_s[:, t, :], in1=mask_col[:, t * TB:(t + 1) * TB], scale=1.0,
                        scalar=3e38, op0=ALU.add, op1=ALU.min, accum_out=ntop[:, t, 0:1]).then_inc(top_ready, 1)

                def own_row(t):
                    nc.vector.tensor_tensor_reduce(
                        out=s_row[:, t, :], in0=ps_s[:, t, t * P:(t + 1) * P], in1=mask_row[:, :], scale=1.0,
                        scalar=3e38, op0=ALU.add, op1=ALU.min, accum_out=ntop[:, t, 1:2]).then_inc(top_ready, 1)

                wait_apart(dve, s_made, 2 * k + j + 1, dve_passed)
                for t in range(2):
                    column(t)
                    own_row(t)

            def sums(k, j):
                i = 2 * k + j
                dve.wait_ge(e_ready, i + 1)
                nc.vector.reciprocal(einv[:, :], esum[:, :]).then_inc(attn_step, 1)

            def probabilities(k, j):
                i = 2 * k + j
                dve.wait_ge(attn_step, 3 * i + 1)
                wait(dve, pT_made, i)
                for t in range(2):
                    nc.vector.tensor_scalar(prob[:, t, :], e_col[:, t, :], einv[:, t:t + 1], None, ALU.mult).then_inc(attn_step, 1)
                for t in range(2):
                    own = prob[:, t, t * P:(t + 1) * P]
                    dve.wait_ge(attn_step, 3 * i + 2 + t)
                    step = nc.vector.scalar_tensor_tensor(own, e_row[:, t, :], einv[:, 2 + t:3 + t], own, ALU.mult, ALU.add)
                step.then_inc(prob_ready, 1)

            def wide(a):
                return a.unsqueeze(2).to_broadcast([P, 2, E])

            def residual(k, j):
                i = 2 * k + j
                dve.wait_ge(o_made, i + 1)
                dve.wait_ge(xb_ready, i + 1)
                if row_of(k, j) is not row_last:
                    dve.wait_ge(row_free, 2 * i + 2)
                nc.vector.tensor_tensor(row_of(k, j)[:, :, 0:D], ps_o[:, :, 0:D], xb[j][:, :, :], ALU.add).then_inc(x2_ready, 1)
                dve.wait_ge(pre_ready, i + 1)
                nc.vector.tensor_tensor(logit[:, :, :], ps_o[:, :, D:VW], pre_logit[j][:, :, :], ALU.add).then_inc(norm_step, 1)


            def shift_logits(k, j):
                i = 2 * k + j
                start = 9 * i
                dve.wait_ge(norm_step, start + 1)
                nc.vector.tensor_reduce(lmax[:, :], logit[:, :, :], axis=AX.X, op=ALU.max).then_inc(norm_step, 1)
                dve.wait_ge(x2_ready, i + 1)
                nc.vector.bn_stats(stats2[:, 0, :], row_of(k, j)[:, 0, 0:D]).then_inc(norm_step, 1)
                dve.wait_ge(norm_step, start + 2)
                nc.vector.tensor_tensor(shifted[:, :, :], logit[:, :, :], wide(lmax[:, :]), ALU.subtract).then_inc(shifted_ready, 1)

            def choose(k, j):
                i = 2 * k + j
                start = 9 * i
                nc.vector.bn_stats(stats2[:, 1, :], row_of(k, j)[:, 1, 0:D]).then_inc(norm_step, 1)
                nc.vector.tensor_copy(row_of(k, j)[:, :, COL_TOK].bitcast(i32), token[:, bass.ds(4 * k + 2 * j, 2)]).then_inc(norm_step, 1)
                dve.wait_ge(norm_step, start + 4)
                dve.wait_ge(shifted_ready, i + 1)
                nc.vector.scalar_tensor_tensor(ranked[:, :, :], shifted[:, :, :], 0.0, rank, ALU.is_equal, ALU.mult).then_inc(norm_step, 1)
                for t in range(2):
                    nc.vector.bn_aggr(mean_var2[:, t, :], stats2[:, t, :]).then_inc(norm_step, 1)
                dve.wait_ge(norm_step, start + 6)
                nc.vector.tensor_reduce(rmax[:, :], ranked[:, :, :], axis=AX.X, op=ALU.max).then_inc(norm_step, 1)
                dve.wait_ge(norm_step, start + 8)
                nc.vector.tensor_scalar(var_eps2[:, :], mean_var2[:, :, 1], EPS_T, None, ALU.add).then_inc(var2_ready, 1)
                dve.wait_ge(norm_step, start + 9)
                nc.vector.tensor_tensor(chosen[:, :, :], rank, wide(rmax[:, :]), ALU.is_equal).then_inc(chosen_ready, 1)

            def place(k, j):
                i = 2 * k + j
                start = 7 * i
                dve.wait_ge(count_made, i + 1)
                nc.vector.tensor_tensor(counted[:, :, :], ps_count, chosen[:, :, :], ALU.mult).then_inc(count_read, 1)
                nc.vector.tensor_tensor(both[:, :], chosen[:, 0, :], chosen[:, 1, :], ALU.add).then_inc(place_step, 1)
                dve.wait_ge(count_read, i + 3)
                nc.vector.tensor_reduce(loc[:, :], counted[:, :, :], axis=AX.X, op=ALU.add).then_inc(place_step, 1)
                dve.wait_ge(rstd2_ready, i + 1)
                nc.vector.scalar_tensor_tensor(row_of(k, j)[:, :, COL_NMR], mean_var2[:, :, 0], -1.0, row_of(k, j)[:, :, COL_RSTD],
                                               ALU.mult, ALU.mult).then_inc(place_step, 1)
                dve.wait_ge(place_step, start + 2)
                nc.vector.tensor_scalar(over[:, :], loc[:, :], float(CAP), float(NOWHERE), ALU.is_gt, ALU.mult).then_inc(place_step, 1)
                nc.vector.scalar_tensor_tensor(place_of[:, :], rmax[:, :], -float(CAP), loc[:, :], ALU.mult, ALU.add).then_inc(place_step, 1)
                nc.vector.tensor_tensor(before[1 - j][:, :], before[j][:, :], both[:, :], ALU.add).then_inc(place_step, 1)

            def finish_rows(k, j):
                i = 2 * k + j
                dve.wait_ge(lexp_ready, i + 1)
                nc.vector.reciprocal(row_of(k, j)[:, :, COL_GATE], gsum[:, :]).then_inc(place_step, 1)
                dve.wait_ge(place_step, 7 * i + 6)
                nc.vector.scalar_tensor_tensor(slot_of(k, j)[:, :], place_of[:, :], float(CAP * E - 1), over[:, :], ALU.add, ALU.add).then_inc(slot_ready, 1)

            def batch(k, j, first=False, second=False, last_but_one=False, last=False):
                if not last:
                    x_low(*after(k, j))
                maxima(k, j)
                if not second:
                    residual(k - 1, j)
                if first:
                    values_low()
                if first:
                    first_norm(4)
                    query_low(*after(k, j))
                elif second:
                    first_norm(5)
                else:
                    shift_logits(k - 1, j)
                    choose(k - 1, j)
                sums(k, j)
                if not first and not last:
                    query_low(*after(k, j))
                probabilities(k, j)
                if first:
                    bias_rows()
                if not second:
                    place(k - 1, j)
                    finish_rows(k - 1, j)
                elif not first:
                    dve.wait_ge(token_in, 16)

            def gathered(k, j):
                e = 2 * k + j
                dve.wait_ge(slots_in[j], 16 * (k + 1))
                for t in range(2):
                    r = 4 * k + 2 * j + t
                    step = nc.vector.tensor_scalar(xs[j][:, t, :], sl[:, bass.ds(r, 1), 0:D], sl[:, bass.ds(r, 1), COL_RSTD:COL_RSTD + 1],
                                                   sl[:, bass.ds(r, 1), COL_NMR:COL_NMR + 1], ALU.mult, ALU.add)
                step.then_inc(xs_ready, 1)

            def output_rows(k, j, last=False):
                e = 2 * k + j
                dve.wait_ge(y_free, e + 1)
                nc.vector.tensor_copy(goal[j][:, :], sl[:, bass.ds(4 * k + 2 * j, 2), COL_TOK].bitcast(i32)).then_inc(goal_ready, 1)
                for t in range(2):
                    if last or t == 0:
                        dve.wait_ge(y_made, e + 1 + t)
                    r = 4 * k + 2 * j + t
                    step = nc.vector.scalar_tensor_tensor(y[j][:, t, :], ps_y_last[t] if last else ps_y[j][:, t, :], sl[:, bass.ds(r, 1), COL_GATE:COL_GATE + 1],
                                                          sl[:, bass.ds(r, 1), 0:D], ALU.mult, ALU.add)
                    if last or t == 1:
                        step.then_inc(y_ready[j], 1)

            def split_w1(n, j):
                for c in range(DC):
                    dve.wait_ge(w1_high_ready, DC * n + c + 1)
                    step = nc.vector.tensor_tensor(w1_low[j][:, c, :], w1_in_sb[:, c, :], w1_high[j][:, c, :].bitcast(f32), ALU.subtract)
                step.then_inc(w1_split, 1)

            def gathered_low(k, j):
                dve.wait_ge(gT_ready, 2 * k + j + 1)
                nc.vector.tensor_tensor(xg_low[j][:, :, :], ps_gT[j], xg_high[j][:, :, :].bitcast(f32), ALU.subtract).then_inc(xg_split, 1)

            def hidden_low(k, j):
                e = 2 * k + j
                for q in range(FC // 2):
                    dve.wait_ge(h_high_ready, (FC // 2) * e + q + 1)
                    nc.vector.scalar_tensor_tensor(h_low[j][:, 2 * q:2 * q + 2, :], ps_h[q], 0.0,
                                                   h_high[j][:, 2 * q:2 * q + 2, :].bitcast(f32), ALU.max, ALU.subtract).then_inc(h_split, 1)

            def expert(k, j, two_on=True):
                if two_on:
                    gathered(k + 1, j)
                hidden_low(*((k, 1) if j == 0 else (k + 1, 0)))
                if two_on:
                    gathered_low(k + 1, j)
                    split_w1(2 * k + j + 2, j)
                output_rows(k, j)

            sweep(dve, batch)
            def last_first_tile():
                dve.wait_ge(o_first_made, 1)
                dve.wait_ge(xb_ready, B)
                nc.vector.tensor_tensor(row_last[:, 0, 0:D], ps_o[:, 0, 0:D], xb[1][:, 0, :], ALU.add).then_inc(norm_step, 1)

            def last_first_stats():
                dve.wait_ge(norm_step, 9 * (B - 1) + 1)
                nc.vector.bn_stats(stats2[:, 0, :], row_last[:, 0, 0:D]).then_inc(norm_step, 1)

            def last_choice():
                start = 9 * (B - 1)
                dve.wait_ge(o_made, B)
                nc.vector.tensor_tensor(row_last[:, 1, 0:D], ps_o[:, 1, 0:D], xb[1][:, 1, :], ALU.add).then_inc(x2_ready, 1)
                nc.vector.tensor_copy(row_last[:, :, COL_TOK].bitcast(i32), token[:, NT - 2:NT]).then_inc(norm_step, 1)
                dve.wait_ge(x2_ready, B)
                nc.vector.bn_stats(stats2[:, 1, :], row_last[:, 1, 0:D]).then_inc(norm_step, 1)
                dve.wait_ge(pre_ready, B)
                nc.vector.tensor_tensor(logit[:, :, :], ps_o[:, :, D:VW], pre_logit[1][:, :, :], ALU.add).then_inc(norm_step, 1)
                dve.wait_ge(norm_step, start + 4)
                for t in range(2):
                    nc.vector.bn_aggr(mean_var2[:, t, :], stats2[:, t, :]).then_inc(norm_step, 1)
                dve.wait_ge(norm_step, start + 5)
                nc.vector.tensor_reduce(lmax[:, :], logit[:, :, :], axis=AX.X, op=ALU.max).then_inc(norm_step, 1)
                dve.wait_ge(norm_step, start + 7)
                nc.vector.tensor_scalar(var_eps2[:, :], mean_var2[:, :, 1], EPS_T, None, ALU.add).then_inc(var2_ready, 1)
                dve.wait_ge(norm_step, start + 8)
                nc.vector.tensor_tensor(shifted[:, :, :], logit[:, :, :], wide(lmax[:, :]), ALU.subtract).then_inc(shifted_ready, 1)
                dve.wait_ge(shifted_ready, B)
                nc.vector.scalar_tensor_tensor(ranked[:, :, :], shifted[:, :, :], 0.0, rank, ALU.is_equal, ALU.mult).then_inc(norm_step, 1)
                dve.wait_ge(norm_step, start + 9)
                nc.vector.tensor_reduce(rmax[:, :], ranked[:, :, :], axis=AX.X, op=ALU.max).then_inc(norm_step, 1)
                dve.wait_ge(norm_step, start + 10)
                nc.vector.tensor_tensor(chosen[:, :, :], rank, wide(rmax[:, :]), ALU.is_equal).then_inc(chosen_ready, 1)

            for part in (residual, shift_logits, choose):
                peeled(B - 2, part)
            last_first_tile()
            peeled(B - 2, place)
            last_first_stats()
            peeled(B - 2, finish_rows)
            last_choice()
            peeled(B - 1, place)
            peeled(B - 1, finish_rows)

            split_w1(1, 1)
            for n in range(2):
                peeled(n, gathered)
            for n in range(2):
                peeled(n, gathered_low)
            peeled(0, hidden_low)
            pairs(dve, 0, E - 3, expert)
            peeled(E - 2, expert, two_on=False)
            peeled(E - 1, output_rows, last=True)


_INS = ["x", "L0_conv_Wq", "L0_conv_bq", "L0_conv_Wk", "L0_conv_bk", "L0_conv_Wv", "L0_conv_bv", "L0_conv_Wo",
        "L0_conv_bo", "L0_conv_sigma", "L0_ffn_wg", "L0_ffn_w1", "L0_ffn_w2"]


def kernel(**inputs):
    import concourse.bacc as bacc
    from concourse.bass_utils import run_bass_kernel_spmd

    nc = bacc.Bacc("TRN2", target_bir_lowering=False, num_devices=1)
    arrays, args = {}, []
    table, ident, token = shape_constants()
    for name, a in [(n, inputs[n]) for n in _INS] + [("tables", table), ("eye", ident), ("tokens", token)]:
        a = np.ascontiguousarray(a)
        arrays[f"in_{name}"] = a
        args.append(nc.dram_tensor(f"in_{name}", a.shape, mybir.dt.from_np(a.dtype), kind="ExternalInput").ap())
    slots = nc.dram_tensor("slots", [N, RW], mybir.dt.float32, kind="Internal").ap()
    out = nc.dram_tensor("out_0", [B, HH, WW, D], mybir.dt.float32, kind="ExternalOutput").ap()
    build(nc, *args, slots, out)
    r = run_bass_kernel_spmd(nc, [arrays], core_ids=[0])
    return r.results[0]["out_0"]
```
